# Optimizing a Trainium2 kernel written in Bass

```python
import numpy as np
import jax
import jax.numpy as jnp

def _softmax(x, axis=-1):
    return jax.nn.softmax(x, axis=axis)

def _gelu(x):
    return jax.nn.gelu(x, approximate=True)

def _silu(x):
    return jax.nn.silu(x)

def _sigmoid(x):
    return jax.nn.sigmoid(x)

def _layernorm(x, axis=-1, eps=1e-05):
    m = jnp.mean(x, axis=axis, keepdims=True)
    v = jnp.var(x, axis=axis, keepdims=True)
    return (x - m) / jnp.sqrt(v + eps)

def _scatter_add(tgt, idx, src, axis=0):
    return tgt.at[idx].add(src)

def _segment_sum(src, seg, n):
    return jax.ops.segment_sum(src, seg, n)
kernel_name = 'mk_vit_tower_cls_d1_tok_img256_r4_68f8a7'

def setup_inputs(seed: int=0):
    np.random.seed(seed)
    _w = jnp.asarray

    def _rec_inputs():
        import jax
        import jax.numpy as jnp
        _rk = jax.random.key(seed)
        x = -0.000125008 + 0.999885 * jax.random.normal(jax.random.fold_in(_rk, 1), (32, 64, 128, 128), jnp.float32)
        cls_tok = 0.02 * jax.random.normal(jax.random.fold_in(_rk, 5), (1, 1, 64), jnp.float32)
        return (x, cls_tok)
    x, cls_tok = _rec_inputs()

    def _L0_tok_setup():
        import jax, jax.numpy as jnp
        import numpy as np
        D_MODEL = 64
        NHEAD = 8
        DS = 4
        OFFSET_SCALE = 4.0

        def bilinear_sample(fm, pts):
            B, C, H, W = fm.shape
            x = (pts[..., 0] + 1.0) * 0.5 * (W - 1)
            y = (pts[..., 1] + 1.0) * 0.5 * (H - 1)
            x0 = jnp.clip(jnp.floor(x), 0.0, W - 2)
            y0 = jnp.clip(jnp.floor(y), 0.0, H - 2)
            wx = jnp.clip(x - x0, 0.0, 1.0)
            wy = jnp.clip(y - y0, 0.0, 1.0)
            x0i = x0.astype(jnp.int32)
            y0i = y0.astype(jnp.int32)
            fm2 = fm.reshape(B, C, H * W)
            N, P = (pts.shape[1], pts.shape[2])

            def gather(yi, xi):
                idx = (yi * W + xi).reshape(B, N * P)
                g = jnp.take_along_axis(fm2, idx[:, None, :], axis=2)
                return g.reshape(B, C, N, P)
            v00 = gather(y0i, x0i)
            v01 = gather(y0i, x0i + 1)
            v10 = gather(y0i + 1, x0i)
            v11 = gather(y0i + 1, x0i + 1)
            wx_ = wx[:, None]
            wy_ = wy[:, None]
            out = v00 * (1 - wx_) * (1 - wy_) + v01 * wx_ * (1 - wy_) + v10 * (1 - wx_) * wy_ + v11 * wx_ * wy_
            return jnp.moveaxis(out, 1, -1)

        def layer_norm(x, g, b, eps=1e-05):
            mu = jnp.mean(x, axis=-1, keepdims=True)
            var = jnp.var(x, axis=-1, keepdims=True)
            return (x - mu) * jax.lax.rsqrt(var + eps) * g + b

        def reference_points(B, H, W):
            yc = jnp.linspace(-1.0, 1.0, H // DS)
            xc = jnp.linspace(-1.0, 1.0, W // DS)
            yg, xg = jnp.meshgrid(yc, xc, indexing='ij')
            ref = jnp.stack([xg.reshape(-1), yg.reshape(-1)], axis=-1)
            return jnp.broadcast_to(ref[None], (B,) + ref.shape)
        key = jax.random.key(seed)
        ks = jax.random.split(key, 6)
        B, C, H, W = (8, D_MODEL, 128, 128)
        s = 0.05
        return {'feature_map': jax.random.normal(ks[0], (B, C, H, W), jnp.float32), 'W_q': jax.random.normal(ks[1], (C, C), jnp.float32) * s, 'W_k': jax.random.normal(ks[2], (C, C), jnp.float32) * s, 'W_v': jax.random.normal(ks[3], (C, C), jnp.float32) * s, 'W_o1': jax.random.normal(ks[4], (C, C // DS), jnp.float32) * s, 'b_o1': jnp.zeros((C // DS,), jnp.float32), 'ln_g': jnp.ones((C // DS,), jnp.float32), 'ln_b': jnp.zeros((C // DS,), jnp.float32), 'W_o2': jax.random.normal(ks[5], (C // DS, NHEAD * 2), jnp.float32) * s, 'b_o2': jnp.zeros((NHEAD * 2,), jnp.float32)}
    _L0_tok_all = _L0_tok_setup()
    _L0_tok_in = {k: v for k, v in _L0_tok_all.items() if k in ('W_q', 'W_k', 'W_v', 'W_o1', 'b_o1', 'ln_g', 'ln_b', 'W_o2', 'b_o2')}
    del _L0_tok_all

    def _L0_attn_setup():
        import jax, jax.numpy as jnp
        import numpy as np
        B, T, C, HR = (8, 1024, 64, 4)
        N_LAYER, LAYER_ID = (12, 3)
        HID = HR * C

        def _fancy_decay_first():
            r01 = LAYER_ID / (N_LAYER - 1)
            h = np.arange(C, dtype=np.float32)
            decay = -5.0 + 8.0 * (h / (C - 1)) ** (0.7 + 1.3 * r01)
            zig = (np.arange(1, C + 1) % 3 - 1).astype(np.float32) * 0.5
            first = np.float32(np.log(0.3)) + zig
            return (jnp.asarray(decay, jnp.float32), jnp.asarray(first, jnp.float32))

        def _ln(x, g, b):
            m = jnp.mean(x, axis=-1, keepdims=True)
            v = jnp.var(x, axis=-1, keepdims=True)
            return (x - m) * jax.lax.rsqrt(v + 1e-05) * g + b

        def _wkv(w, u, k, v):
            Bb, Tt, Cc = k.shape
            kT = jnp.swapaxes(k, 0, 1)
            vT = jnp.swapaxes(v, 0, 1)

            def step(carry, kv):
                p, q, o = carry
                kt, vt = kv
                no = jnp.maximum(o, u + kt)
                A = jnp.exp(o - no)
                E = jnp.exp(u + kt - no)
                y = (A * p + E * vt) / (A * q + E)
                no2 = jnp.maximum(w + o, kt)
                A2 = jnp.exp(w + o - no2)
                E2 = jnp.exp(kt - no2)
                return ((A2 * p + E2 * vt, A2 * q + E2, no2), y)
            init = (jnp.zeros((Bb, Cc), k.dtype), jnp.zeros((Bb, Cc), k.dtype), jnp.full((Bb, Cc), -1e+38, k.dtype))
            _, yT = jax.lax.scan(step, init, (kT, vT))
            return jnp.swapaxes(yT, 0, 1)
        key = jax.random.key(seed)
        ks = jax.random.split(key, 12)
        s = 0.02
        decay, first = _fancy_decay_first()
        return {'x': jax.random.normal(ks[0], (B, T, C), jnp.float32), 'Wk': jax.random.normal(ks[1], (C, C), jnp.float32) * s, 'Wv': jax.random.normal(ks[2], (C, C), jnp.float32) * s, 'Wr': jax.random.normal(ks[3], (C, C), jnp.float32) * s, 'Wo': jax.random.normal(ks[4], (C, C), jnp.float32) * s, 'Wk_ffn': jax.random.normal(ks[5], (C, HID), jnp.float32) * s, 'Wv_ffn': jax.random.normal(ks[6], (HID, C), jnp.float32) * s, 'Wr_ffn': jax.random.normal(ks[7], (C, C), jnp.float32) * s, 'g1': 1.0 + 0.1 * jax.random.normal(ks[8], (C,), jnp.float32), 'b1': 0.1 * jax.random.normal(ks[9], (C,), jnp.float32), 'g2': 1.0 + 0.1 * jax.random.normal(ks[10], (C,), jnp.float32), 'b2': 0.1 * jax.random.normal(ks[11], (C,), jnp.float32), 'spatial_decay': decay, 'spatial_first': first}
    _L0_attn_all = _L0_attn_setup()
    _L0_attn_in = {k: v for k, v in _L0_attn_all.items() if k in ('Wk', 'Wv', 'Wr', 'Wo', 'Wk_ffn', 'Wv_ffn', 'Wr_ffn', 'g1', 'b1', 'g2', 'b2', 'spatial_decay', 'spatial_first')}
    del _L0_attn_all

    def _L0_ffn_setup():
        import jax, jax.numpy as jnp
        import numpy as np
        B, K, D = (128, 16, 64)
        E = 32
        H = int(D * 0.25)
        key = jax.random.key(seed)
        ks = jax.random.split(key, 7)
        d_rs = D ** (-0.5)
        h_rs = H ** (-0.5)
        x = jax.random.normal(ks[0], (B, K, D), dtype=jnp.float32)
        router_w = jax.random.uniform(ks[1], (E, D), jnp.float32, -d_rs, d_rs)
        router_b = jax.random.uniform(ks[2], (E,), jnp.float32, -d_rs, d_rs)
        W1 = jax.random.uniform(ks[3], (E, D, H), jnp.float32, -h_rs, h_rs)
        b1 = jax.random.uniform(ks[4], (E, H), jnp.float32, -h_rs, h_rs)
        W2 = jax.random.uniform(ks[5], (E, H, D), jnp.float32, -d_rs, d_rs)
        b2 = jax.random.uniform(ks[6], (E, D), jnp.float32, -d_rs, d_rs)
        return {'x': x, 'router_w': router_w, 'router_b': router_b, 'W1': W1, 'b1': b1, 'W2': W2, 'b2': b2}
    _L0_ffn_all = _L0_ffn_setup()
    _L0_ffn_in = {k: v for k, v in _L0_ffn_all.items() if k in ('router_w', 'router_b', 'W1', 'b1', 'W2', 'b2')}
    del _L0_ffn_all
    return {'x': x, 'cls_tok': cls_tok, 'L0_tok_W_q': _L0_tok_in['W_q'], 'L0_tok_W_k': _L0_tok_in['W_k'], 'L0_tok_W_v': _L0_tok_in['W_v'], 'L0_tok_W_o1': _L0_tok_in['W_o1'], 'L0_tok_b_o1': _L0_tok_in['b_o1'], 'L0_tok_ln_g': _L0_tok_in['ln_g'], 'L0_tok_ln_b': _L0_tok_in['ln_b'], 'L0_tok_W_o2': _L0_tok_in['W_o2'], 'L0_tok_b_o2': _L0_tok_in['b_o2'], 'L0_attn_Wk': _L0_attn_in['Wk'], 'L0_attn_Wv': _L0_attn_in['Wv'], 'L0_attn_Wr': _L0_attn_in['Wr'], 'L0_attn_Wo': _L0_attn_in['Wo'], 'L0_attn_Wk_ffn': _L0_attn_in['Wk_ffn'], 'L0_attn_Wv_ffn': _L0_attn_in['Wv_ffn'], 'L0_attn_Wr_ffn': _L0_attn_in['Wr_ffn'], 'L0_attn_g1': _L0_attn_in['g1'], 'L0_attn_b1': _L0_attn_in['b1'], 'L0_attn_g2': _L0_attn_in['g2'], 'L0_attn_b2': _L0_attn_in['b2'], 'L0_attn_spatial_decay': _L0_attn_in['spatial_decay'], 'L0_attn_spatial_first': _L0_attn_in['spatial_first'], 'L0_ffn_router_w': _L0_ffn_in['router_w'], 'L0_ffn_router_b': _L0_ffn_in['router_b'], 'L0_ffn_W1': _L0_ffn_in['W1'], 'L0_ffn_b1': _L0_ffn_in['b1'], 'L0_ffn_W2': _L0_ffn_in['W2'], 'L0_ffn_b2': _L0_ffn_in['b2']}

def reference(x, cls_tok, L0_tok_W_q, L0_tok_W_k, L0_tok_W_v, L0_tok_W_o1, L0_tok_b_o1, L0_tok_ln_g, L0_tok_ln_b, L0_tok_W_o2, L0_tok_b_o2, L0_attn_Wk, L0_attn_Wv, L0_attn_Wr, L0_attn_Wo, L0_attn_Wk_ffn, L0_attn_Wv_ffn, L0_attn_Wr_ffn, L0_attn_g1, L0_attn_b1, L0_attn_g2, L0_attn_b2, L0_attn_spatial_decay, L0_attn_spatial_first, L0_ffn_router_w, L0_ffn_router_b, L0_ffn_W1, L0_ffn_b1, L0_ffn_W2, L0_ffn_b2):
    import jax
    import jax.numpy as jnp

    def _L0_tok_ref(feature_map, W_q, W_k, W_v, W_o1, b_o1, ln_g, ln_b, W_o2, b_o2):
        import jax, jax.numpy as jnp
        import numpy as np
        D_MODEL = 64
        NHEAD = 8
        DS = 4
        OFFSET_SCALE = 4.0

        def bilinear_sample(fm, pts):
            B, C, H, W = fm.shape
            x = (pts[..., 0] + 1.0) * 0.5 * (W - 1)
            y = (pts[..., 1] + 1.0) * 0.5 * (H - 1)
            x0 = jnp.clip(jnp.floor(x), 0.0, W - 2)
            y0 = jnp.clip(jnp.floor(y), 0.0, H - 2)
            wx = jnp.clip(x - x0, 0.0, 1.0)
            wy = jnp.clip(y - y0, 0.0, 1.0)
            x0i = x0.astype(jnp.int32)
            y0i = y0.astype(jnp.int32)
            fm2 = fm.reshape(B, C, H * W)
            N, P = (pts.shape[1], pts.shape[2])

            def gather(yi, xi):
                idx = (yi * W + xi).reshape(B, N * P)
                g = jnp.take_along_axis(fm2, idx[:, None, :], axis=2)
                return g.reshape(B, C, N, P)
            v00 = gather(y0i, x0i)
            v01 = gather(y0i, x0i + 1)
            v10 = gather(y0i + 1, x0i)
            v11 = gather(y0i + 1, x0i + 1)
            wx_ = wx[:, None]
            wy_ = wy[:, None]
            out = v00 * (1 - wx_) * (1 - wy_) + v01 * wx_ * (1 - wy_) + v10 * (1 - wx_) * wy_ + v11 * wx_ * wy_
            return jnp.moveaxis(out, 1, -1)

        def layer_norm(x, g, b, eps=1e-05):
            mu = jnp.mean(x, axis=-1, keepdims=True)
            var = jnp.var(x, axis=-1, keepdims=True)
            return (x - mu) * jax.lax.rsqrt(var + eps) * g + b

        def reference_points(B, H, W):
            yc = jnp.linspace(-1.0, 1.0, H // DS)
            xc = jnp.linspace(-1.0, 1.0, W // DS)
            yg, xg = jnp.meshgrid(yc, xc, indexing='ij')
            ref = jnp.stack([xg.reshape(-1), yg.reshape(-1)], axis=-1)
            return jnp.broadcast_to(ref[None], (B,) + ref.shape)
        B, C, H, W = feature_map.shape
        dh = C // NHEAD
        ref = reference_points(B, H, W)
        Nq = ref.shape[1]
        q_feat = bilinear_sample(feature_map, ref[:, :, None, :])[:, :, 0]
        queries = q_feat @ W_q.T
        h = jax.nn.gelu(layer_norm(q_feat @ W_o1 + b_o1, ln_g, ln_b))
        off = (h @ W_o2 + b_o2).reshape(B, Nq, NHEAD, 2) * OFFSET_SCALE
        scale = jnp.array([2.0 / (W - 1), 2.0 / (H - 1)], jnp.float32)
        sampling_points = ref[:, :, None, :] + off * scale
        sampled = bilinear_sample(feature_map, sampling_points)
        keys = jnp.einsum('bnpc,dc->bnpd', sampled, W_k)
        values = jnp.einsum('bnpc,dc->bnpd', sampled, W_v)
        q = queries.reshape(B, Nq, NHEAD, dh)
        k = keys.reshape(B, Nq, NHEAD, NHEAD, dh)
        v = values.reshape(B, Nq, NHEAD, NHEAD, dh)
        scores = jnp.einsum('bnhd,bnphd->bnhp', q, k) / jnp.sqrt(jnp.float32(dh))
        attn = jax.nn.softmax(scores, axis=-1)
        out = jnp.einsum('bnhp,bnphd->bnhd', attn, v).reshape(B, Nq, C)
        return out

    def _L0_attn_ref(x, Wk, Wv, Wr, Wo, Wk_ffn, Wv_ffn, Wr_ffn, g1, b1, g2, b2, spatial_decay, spatial_first):
        import jax, jax.numpy as jnp
        import numpy as np
        B, T, C, HR = (8, 1024, 64, 4)
        N_LAYER, LAYER_ID = (12, 3)
        HID = HR * C

        def _fancy_decay_first():
            r01 = LAYER_ID / (N_LAYER - 1)
            h = np.arange(C, dtype=np.float32)
            decay = -5.0 + 8.0 * (h / (C - 1)) ** (0.7 + 1.3 * r01)
            zig = (np.arange(1, C + 1) % 3 - 1).astype(np.float32) * 0.5
            first = np.float32(np.log(0.3)) + zig
            return (jnp.asarray(decay, jnp.float32), jnp.asarray(first, jnp.float32))

        def _ln(x, g, b):
            m = jnp.mean(x, axis=-1, keepdims=True)
            v = jnp.var(x, axis=-1, keepdims=True)
            return (x - m) * jax.lax.rsqrt(v + 1e-05) * g + b

        def _wkv(w, u, k, v):
            Bb, Tt, Cc = k.shape
            kT = jnp.swapaxes(k, 0, 1)
            vT = jnp.swapaxes(v, 0, 1)

            def step(carry, kv):
                p, q, o = carry
                kt, vt = kv
                no = jnp.maximum(o, u + kt)
                A = jnp.exp(o - no)
                E = jnp.exp(u + kt - no)
                y = (A * p + E * vt) / (A * q + E)
                no2 = jnp.maximum(w + o, kt)
                A2 = jnp.exp(w + o - no2)
                E2 = jnp.exp(kt - no2)
                return ((A2 * p + E2 * vt, A2 * q + E2, no2), y)
            init = (jnp.zeros((Bb, Cc), k.dtype), jnp.zeros((Bb, Cc), k.dtype), jnp.full((Bb, Cc), -1e+38, k.dtype))
            _, yT = jax.lax.scan(step, init, (kT, vT))
            return jnp.swapaxes(yT, 0, 1)
        Tlen = x.shape[1]
        h = _ln(x, g1, b1)
        k = h @ Wk
        v = h @ Wv
        sr = jax.nn.sigmoid(h @ Wr)
        y = _wkv(spatial_decay / Tlen, spatial_first / Tlen, k, v)
        x = x + sr * y @ Wo
        h2 = _ln(x, g2, b2)
        kk = jnp.square(jax.nn.relu(h2 @ Wk_ffn))
        x = x + jax.nn.sigmoid(h2 @ Wr_ffn) * (kk @ Wv_ffn)
        return x

    def _L0_ffn_ref(x, router_w, router_b, W1, b1, W2, b2):
        import jax, jax.numpy as jnp
        import numpy as np
        B, K, D = (128, 16, 64)
        E = 32
        H = int(D * 0.25)
        xf = x.reshape(-1, D)
        logits = xf @ router_w.T + router_b
        idx = jnp.argmax(logits, axis=-1)
        w1t = jnp.take(W1, idx, axis=0)
        h = jnp.einsum('nd,ndh->nh', xf, w1t) + jnp.take(b1, idx, axis=0)
        h = jax.nn.relu(h)
        w2t = jnp.take(W2, idx, axis=0)
        out = jnp.einsum('nh,nhd->nd', h, w2t) + jnp.take(b2, idx, axis=0)
        out = jax.nn.relu(out)
        return out.reshape(x.shape)
    h = _L0_tok_ref(x, L0_tok_W_q, L0_tok_W_k, L0_tok_W_v, L0_tok_W_o1, L0_tok_b_o1, L0_tok_ln_g, L0_tok_ln_b, L0_tok_W_o2, L0_tok_b_o2)
    h = jnp.concatenate([jnp.broadcast_to(cls_tok, (h.shape[0], 1, h.shape[2])), h], axis=1)
    h = h + _L0_attn_ref(_layernorm(h, axis=-1), L0_attn_Wk, L0_attn_Wv, L0_attn_Wr, L0_attn_Wo, L0_attn_Wk_ffn, L0_attn_Wv_ffn, L0_attn_Wr_ffn, L0_attn_g1, L0_attn_b1, L0_attn_g2, L0_attn_b2, L0_attn_spatial_decay, L0_attn_spatial_first)
    h = h + _L0_ffn_ref(_layernorm(h, axis=-1), L0_ffn_router_w, L0_ffn_router_b, L0_ffn_W1, L0_ffn_b1, L0_ffn_W2, L0_ffn_b2)
    return h

_drawn_inputs = setup_inputs


def setup_inputs(seed=0):
    import zlib

    import numpy as np

    out = dict(_drawn_inputs(seed))
    spreads = {'L0_tok_b_o1': (0.0, 0.1),
     'L0_tok_ln_g': (1.0, 0.2),
     'L0_tok_ln_b': (0.0, 0.1),
     'L0_tok_b_o2': (0.0, 0.1)}
    factors = {'L0_attn_Wk': 8.0,
     'L0_attn_Wv': 8.0,
     'L0_attn_Wr': 8.0,
     'L0_attn_Wo': 8.0,
     'L0_attn_Wk_ffn': 5.512,
     'L0_attn_Wv_ffn': 5.336,
     'L0_attn_Wr_ffn': 8.0,
     'L0_attn_g1': 8.0,
     'L0_attn_b1': 8.0,
     'L0_attn_g2': 8.0,
     'L0_attn_b2': 8.0,
     'L0_attn_spatial_decay': 8.0,
     'L0_attn_spatial_first': 200.0,
     'L0_ffn_b1': 28.288,
     'L0_ffn_router_w': 8.0,
     'L0_ffn_router_b': 8.0,
     'L0_ffn_W1': 8.0,
     'L0_ffn_W2': 8.0,
     'L0_ffn_b2': 64.0}
    for name, (base, spread) in spreads.items():
        noise = np.random.default_rng([zlib.crc32(name.encode()), seed]).standard_normal(out[name].shape)
        drawn = base * np.exp(spread * noise) if base else spread * noise
        out[name] = jnp.asarray(drawn.astype(out[name].dtype))
    for name, factor in factors.items():
        out[name] = (out[name] * factor).astype(out[name].dtype)
    return out
```

```python
from contextlib import ExitStack

import numpy as np

import concourse.bass as bass
from concourse import mybir

ALU = mybir.AluOpType
ACT = mybir.ActivationFunctionType
AX_X = mybir.AxisListType.X
F32 = mybir.dt.float32
BF16 = mybir.dt.bfloat16
I32 = mybir.dt.int32

P = 128
C = 64
SIDE = 128
GRID = 32
NQ = GRID * GRID
TILES = NQ // P
HEADS = 8
DH = C // HEADS
OFF = 16
PATCH = 4 * C
PAIR_TILES = 2 * TILES
SEQ = NQ + 1
HALF = NQ // 2
HID = 4 * C
EXPERTS = 32
EH = 16
BLOCKS = EXPERTS * EH // P
IMAGE_ROWS = (SIDE - 1) * SIDE
RING = 4
MASKED = 3.0e38
EPS = 1e-5

W_KV, W_QO, W_O2, W_K, W_V, W_R, W_O, W_FR, W_RT, W_B2 = range(10)
W_UP, W_DN, W_MU, W_MD = 10, 14, 18, 26
N_WEIGHTS = 34
C_IDENT, C_CENTER, C_MEAN, C_SEL = 0, 1, 2, 3
N_CONSTS = 3 + 2 * BLOCKS

V_G1, V_B1, V_G2, V_B2, V_U, V_W, V_MB1 = 0, 1, 2, 3, 4, 5, 6
V_BO1 = 10
V_LNG, V_LNB, V_BO2, V_RB = V_BO1 + OFF, V_BO1 + 2 * OFF, V_BO1 + 3 * OFF, V_BO1 + 4 * OFF
N_VECTORS = V_RB + EXPERTS
S_GW, S_BASE, S_RANK = 0, TILES * 4, TILES * (4 + 2 * HEADS)
N_SHAPE_VECTORS = S_RANK + EXPERTS

SCHEDULE = [
    (0, 1, ["in0"]), (0, 1, ["cena0"]), (1, 1, ["vara0"]),
    (1, 2, ["cenm0", "cenm1"]), (2, 2, ["varm0", "varm1"]),
    (3, 1, ["k0", "v0", "r0"]),
    (4, 2, ["route0", "route1"]),
    (5, 1, ["in1"]), (5, 1, ["cena1"]), (6, 1, ["vara1"]),
    (6, "q0", ["qt0", "qt1"]), (7, "q0", ["qo0", "qo1"]),
    (7, 2, ["one0", "one1"]),
    (8, 1, ["k1", "v1", "r1"]),
    (9, 2, ["mu0.0", "mu0.1"]), (10, 2, ["mu0.2", "mu0.3"]),
    (11, 2, ["mu0.4", "mu0.5"]), (12, 2, ["mu0.6", "mu0.7"]),
    (13, "q0", ["ht"]), (13, "q0", ["of"]),
    (14, 2, ["md0"]),
    (15, 2, ["mu1.0", "mu1.1"]), (16, 2, ["mu1.2", "mu1.3"]),
    (17, 2, ["mu1.4", "mu1.5"]), (18, 2, ["mu1.6", "mu1.7"]),
    (20, 2, ["md1"]),
    (21, 1, ["wo0", "wo1"]),
    (22, 2, ["out0"]), (23, 2, ["out1"]),
    (24, 1, ["cenf0", "cenf1"]), (25, 1, ["varf0", "varf1"]),
    (28, 1, ["up0.0", "up0.1"]), (29, 1, ["up0.2", "up0.3"]),
    (30, 1, ["up1.0", "up1.1"]), (31, 1, ["up1.2", "up1.3"]),
    (32, "q1", ["qt0", "qt1"]),
    (33, 1, ["gate0", "gate1"]), (33, "q1", ["qo0", "qo1"]),
    (34, 1, ["dn0"]), (36, 1, ["dn1"]),
    (39, "q1", ["ht"]), (39, "q1", ["of"]),
]
VECTOR_AT = {
    "mix_input0": 2, "mix_input1": 7, "running_max": 9, "running_sums": 13, "mixed_sums": 16, "mixed": 17,
    "add_mix": 22, "ffn_input": 27, "gate": 34, "add_ffn0": 35, "add_ffn1": 38,
    "moe_input": 3, "take_logits": 5, "choose": 6, "add_moe0": 15, "add_moe1": 21,
    "grid_corners0": 4, "features0": 8, "normalised0": 10, "gelu0": 12, "sampling_points0": 14,
    "grid_corners1": 30, "features1": 34, "normalised1": 36, "gelu1": 38, "sampling_points1": 40,
}
SCALAR_AT = {"update": 10, "output": 12, "feature_std0": 9, "gelu_exp0": 11, "feature_std1": 35, "gelu_exp1": 37}
COMMIT_AT = (27, 3)
ROUND = float(2 ** 23)


def work_uses(parts):
    names = [(part, name) for _, part, group in SCHEDULE if part in parts for name in group]
    return {key: n for n, key in enumerate(names)}, len(names)


class Signal:

    def __init__(self, sem, per):
        self.sem, self.per = sem, per

    def at(self, run, n):
        value = run * self.per + n
        return max(value, 0) if isinstance(run, int) else value


class Steps:

    def __init__(self, sem, per_loop):
        self.sem, self.per, self.count, self.loop = sem, per_loop, 0, None

    def mark(self, ins):
        ins.then_inc(self.sem, 1)
        self.count += 1
        return self.count

    def value(self, n):
        return n if self.loop is None else n + self.loop * self.per

    def enter(self, turn):
        self.loop, self.start = turn, self.count

    def leave(self, turns):
        assert self.count - self.start == self.per, (self.count - self.start, self.per)
        self.loop, self.count = None, self.start + turns * self.per


def vit_kernel(nc, pixels, grid, cls, weights, vectors, consts, shape_vectors, out):
    images = out.shape[0]
    pairs = images // 2
    first_looped, last_looped = 2, pairs - 2
    VECTOR_STEPS, SCALAR_STEPS = 185, 12

    all_parts = (1, 2, "q0", "q1")
    position, per_iteration = {}, {}
    for parts in (("q0", "q1"), (1, "q0", "q1"), all_parts, (1, 2), (2,)):
        position[parts], per_iteration[parts] = work_uses(parts)

    def parts_of(it):
        if not isinstance(it, int):
            return all_parts
        if it < 0:
            return ("q0", "q1")
        parts = ((1,) if it <= pairs else ()) + ((2,) if it > 0 else ())
        return parts + (("q0", "q1") if it < pairs - 1 else ())

    def uses_before(it):
        if not isinstance(it, int):
            return (it - first_looped) * per_iteration[all_parts] + uses_before(first_looped)
        return sum(per_iteration[parts_of(x)] for x in range(-1, it))

    def bank_of(it, part, name):
        n = position[parts_of(it)][(part, name)]
        if isinstance(it, int):
            n += uses_before(it)
            return n % 2, n // 2
        before = (it - first_looped) * (per_iteration[all_parts] // 2) + uses_before(first_looped) // 2
        return n % 2, before + n // 2

    with ExitStack() as ctx:
        def sb(name, shape, dt=F32):
            return ctx.enter_context(nc.sbuf_tensor(name, shape, dt))

        def signal(name, per=1):
            return Signal(ctx.enter_context(nc.semaphore(name)), per)

        w_sb = sb("w_sb", [P, N_WEIGHTS, P])
        c_sb = sb("c_sb", [P, 3, P])
        sel_sb = sb("sel_sb", [P, 2 * BLOCKS, P], BF16)
        v_sb = sb("v_sb", [P, N_VECTORS])
        s_sb = sb("s_sb", [P, N_SHAPE_VECTORS])
        small = sb("small", [P, 3])
        eps_col, eps2_col, minus1_col = small[:, 0:1], small[:, 1:2], small[:, 2:3]
        fold = sb("fold", [P, 8])
        decay = sb("decay", [P, 4])
        image_base = sb("image_base", [P, 1])
        gathered = sb("gathered", [P, RING, HEADS * PATCH])
        sampled_t = sb("sampled_t", [P, 2, HEADS, P])
        qk = sb("qk", [P, HEADS, C])
        av = sb("av", [P, HEADS, C])
        scores = sb("scores", [P, HEADS, HEADS])
        shifted = sb("shifted", [P, HEADS, HEADS])
        top = sb("top", [P, HEADS])
        probs = sb("probs", [P, 2, HEADS, HEADS])
        prob_sum = sb("prob_sum", [P, HEADS])
        attended_raw = sb("attended_raw", [P, C])
        attended = sb("attended", [P, TILES, 2, C])
        grid_px = sb("grid_px", [P, TILES, PATCH])
        grid_t = sb("grid_t", [P, TILES, P])
        qo_tmp = sb("qo_tmp", [P, TILES, C + OFF])
        feat_a = sb("feat_a", [P, TILES, OFF])
        feat_b = sb("feat_b", [P, TILES, OFF])
        feat_c = sb("feat_c", [P, TILES, OFF])
        feat_s = sb("feat_s", [P, 2, TILES])
        feat_r = sb("feat_r", [P, 2, TILES])
        hid_t = sb("hid_t", [P, P])
        frac = sb("frac", [P, TILES, HEADS, 2])
        corner = sb("corner", [P, TILES, HEADS, 2])
        queries = sb("queries", [P, 2, TILES, C])
        mix = sb("mix", [P, 2, TILES, HEADS, 4])
        index = sb("index", [P, 2, TILES * HEADS], I32)
        h0 = sb("h0", [P, NQ])
        xc = sb("xc", [P, NQ])
        rs1 = sb("rs1", [P, NQ])
        rs2 = sb("rs2", [P, NQ])
        x1 = sb("x1", [P, NQ])
        hn = sb("hn", [P, NQ])
        state_o = sb("state_o", [P, NQ + 1])
        state_p = sb("state_p", [P, NQ + 1])
        state_q = sb("state_q", [P, NQ + 1])
        wide = sb("wide", [P, 4, NQ])
        hidden = wide[:, :, :].rearrange("p a (h n) -> p (a h) n", h=2)
        hm = sb("hm", [P, NQ])
        xm = sb("xm", [P, NQ])
        rm = sb("rm", [P, NQ])
        nm = sb("nm", [P, NQ])
        logits = sb("logits", [P, TILES, 2, EXPERTS])
        logit_top = sb("logit_top", [P, TILES, 2])
        choice = sb("choice", [P, TILES, P])
        choice_t = sb("choice_t", [P, NQ])
        others_t = sb("others_t", [P, NQ], BF16)
        moe_hidden = sb("moe_hidden", [P, 2 * BLOCKS, HALF])
        sel_stage = moe_hidden[:, 0:2, :].rearrange("p a (s n) -> p (a s) n", n=P)

        points_ps = ctx.enter_context(nc.psum_tensor("points_ps", [P, 2, 512], F32))
        kv_ps = ctx.enter_context(nc.psum_tensor("kv_ps", [P, 4, 512], F32))
        work_ps = ctx.enter_context(nc.psum_tensor("work_ps", [P, 2, 512], F32))

        loaded = signal("loaded")
        cls_loaded = signal("cls_loaded")
        sel_cast = signal("sel_cast")
        filled = signal("filled")
        bias_full = signal("bias_full")
        bias_read = signal("bias_read")
        folded = signal("folded")
        slot_gathered = [signal(f"slot_gathered{k}", PAIR_TILES // RING * HEADS * 16) for k in range(RING)]
        tiles_started = signal("tiles_started", PAIR_TILES)
        weighted = signal("weighted", PAIR_TILES)
        points_full = signal("points_full", 2 * PAIR_TILES)
        points_copied = signal("points_copied", 2 * PAIR_TILES)
        kv_full = signal("kv_full", 2 * PAIR_TILES)
        scores_ready = signal("scores_ready", PAIR_TILES)
        probs_ready = signal("probs_ready", PAIR_TILES)
        values_used = signal("values_used", PAIR_TILES)
        attended_ready = signal("attended_ready", PAIR_TILES)
        grid_loaded = signal("grid_loaded", 32)
        grid_summed = signal("grid_summed", 2)
        feature_var = signal("feature_var", 2)
        feature_std = signal("feature_std", 2)
        gelu_arg = signal("gelu_arg", 2)
        gelu_exp = signal("gelu_exp", 2)
        gelu_ready = signal("gelu_ready", 2)
        index_ready = signal("index_ready", 2)
        queries_ready = signal("queries_ready", 2)
        bank_full = [signal(f"bank_full{k}") for k in range(2)]
        bank_read = [signal(f"bank_read{k}") for k in range(2)]
        stds_a = signal("stds_a", 2)
        mix_in_ready = signal("mix_in_ready", 2)
        diff_ready = signal("diff_ready")
        update_gates = signal("update_gates")
        output_gates = signal("output_gates")
        mixed_ready = signal("mixed_ready")
        stds_f = signal("stds_f", 2)
        ffn_in_ready = signal("ffn_in_ready", 2)
        hidden_ready = signal("hidden_ready", 8)
        hm_ready = signal("hm_ready", 2)
        stds_m = signal("stds_m", 2)
        nm_ready = signal("nm_ready", 2)
        choice_ready = signal("choice_ready")
        written = signal("written", 32)
        vector_steps = Steps(ctx.enter_context(nc.semaphore("vector_steps")), VECTOR_STEPS)
        scalar_steps = Steps(ctx.enter_context(nc.semaphore("scalar_steps")), SCALAR_STEPS)

        ident = c_sb[:, C_IDENT, :]
        block = ctx.enter_context(nc.Block())

        def cols(h):
            return slice(h * HALF, (h + 1) * HALF)

        def fill(eng, it, part, name):
            k, before = bank_of(it, part, name)
            eng.wait_ge(bank_read[k].sem, before)
            return work_ps[:, k, :], bank_full[k].sem

        def full(eng, it, part, name):
            k, before = bank_of(it, part, name)
            eng.wait_ge(bank_full[k].sem, before + 1)
            return work_ps[:, k, :], bank_read[k].sem

        def was_read(eng, it, part, name):
            k, before = bank_of(it, part, name)
            eng.wait_ge(bank_read[k].sem, before + 1)

        def all_iterations(eng, iteration, steps=None):
            for it in range(min(first_looped, pairs)):
                iteration(it)
            if last_looped >= first_looped:
                with eng.Fori(first_looped, last_looped + 1) as it:
                    if steps:
                        steps.enter(it - first_looped)
                    iteration(it)
                if steps:
                    steps.leave(last_looped + 1 - first_looped)
            for it in range(max(last_looped + 1, first_looped), pairs + 2):
                iteration(it)

        def samples_in(it):
            return not isinstance(it, int) or it < pairs

        def stages(it, j):
            return [(part, names) for slot, part, names in SCHEDULE if slot == j and part in parts_of(it)]

        @block.sync
        def _(sp):
            sp.dma_start(w_sb[:, :, :], weights).then_inc(loaded.sem, 16)
            sp.dma_start(v_sb[:, :], vectors).then_inc(loaded.sem, 16)
            sp.dma_start(c_sb[:, :, :], consts[:, 0:3, :]).then_inc(loaded.sem, 16)
            sp.dma_start(sel_stage, consts[:, C_SEL:N_CONSTS, :]).then_inc(loaded.sem, 16)
            sp.dma_start(s_sb[:, :], shape_vectors).then_inc(loaded.sem, 16)

            def load_grid(it, b):
                if b == 1:
                    was_read(sp, it, "q0", "qt1")
                elif not isinstance(it, int) or it >= 0:
                    was_read(sp, it - 1, "q1", "qt1")
                sp.dma_start(grid_px[:, :, :].rearrange("p t n -> p (t n)"),
                             grid[2 * (it + 1) + b, :, :]).then_inc(grid_loaded.sem, 16)

            def store(it):
                was_read(sp, it, 2, "out0")
                was_read(sp, it, 2, "out1")
                if isinstance(it, int) and it == 1:
                    for b in range(2):
                        to = out[b * (images // 2):(b + 1) * (images // 2), 0:1, :].rearrange("b o c -> o b c")
                        sp.dma_start(to, rm[0:1, 0:C].unsqueeze(1).broadcast_to([1, images // 2, C])).then_inc(written.sem, 16)
                else:
                    for b in range(2):
                        to = out[2 * (it - 2) + b, 1:SEQ, :].rearrange("(t p) c -> p t c", p=P)
                        sp.dma_start(to, rm[:, :].rearrange("p (t b c) -> p t b c", t=TILES, b=2)[:, :, b, :]
                                     ).then_inc(written.sem, 16)

            def iteration(it):
                parts = parts_of(it)
                for b in range(2):
                    if "q0" in parts:
                        load_grid(it, b)
                if 2 in parts:
                    store(it)

            load_grid(-1, 0)
            sp.dma_start(attended[:, :, :, :].rearrange("p t b c -> p (t b) c"),
                         cls.unsqueeze(1).broadcast_to([P, 2 * TILES, C])).then_inc(cls_loaded.sem, 16)
            load_grid(-1, 1)
            all_iterations(sp, iteration)
            sp.wait_ge(written.sem, written.at(pairs, 32))

        @block.gpsimd
        def _(pool):
            def iteration(it):
                if not samples_in(it):
                    return
                for n in range(PAIR_TILES):
                    if n % TILES == 0:
                        pool.wait_ge(index_ready.sem, index_ready.at(it, n // TILES + 1))
                    pool.wait_ge(points_full.sem, points_full.at(it, 2 * (n - RING) + 2))
                    pool.sem_inc(tiles_started.sem, 1)
                    for k in range(HEADS):
                        at = (n % TILES) * HEADS + k
                        pool.indirect_dma_start(
                            gathered[:, n % RING, k * PATCH:(k + 1) * PATCH], None, pixels,
                            bass.IndirectOffsetOnAxis(ap=index[:, n // TILES, at:at + 1], axis=0),
                        ).then_inc(slot_gathered[n % RING].sem, 16)

            all_iterations(pool, iteration)

        @block.tensor
        def _(pe):
            def w(n):
                return w_sb[:, n, :]

            def product(it, part, name, lhsT, rhs):
                bank, filled_now = fill(pe, it, part, name)
                pe.matmul(bank, lhsT, rhs, start=True, stop=True).then_inc(filled_now, 1)

            pe.wait_ge(loaded.sem, 16 * 5)
            for n, (m, shift) in enumerate([(W_K, V_B1), (W_V, V_B1), (W_R, V_B1), (W_FR, V_B2),
                                            (W_UP, V_B2), (W_UP + 1, V_B2),
                                            (W_UP + 2, V_B2), (W_UP + 3, V_B2)]):
                mm = pe.matmul(work_ps[:, 0, n:n + 1], w(m), v_sb[:, shift:shift + 1], start=True, stop=True)
            mm.then_inc(bias_full.sem, 1)
            pe.wait_ge(bias_read.sem, 1)
            pe.wait_ge(folded.sem, 1)
            pe.wait_ge(sel_cast.sem, 1)
            pe.wait_ge(filled.sem, 1)

            def prepare(it, part, name):
                b, run = int(part[1]), it + 1
                if name == "qt0":
                    pe.wait_ge(grid_summed.sem, grid_summed.at(run, b + 1))
                    for h in range(2):
                        bank, done = fill(pe, it, part, f"qt{h}")
                        for t in range(4):
                            mm = pe.transpose(bank[:, t * P:(t + 1) * P], grid_px[:, 4 * h + t, 0:2 * C], ident)
                        mm.then_inc(done, 1)
                if name == "qo0":
                    for h in range(2):
                        bank, done = fill(pe, it, part, f"qo{h}")
                        was_read(pe, it, part, f"qt{h}")
                        for t in range(4):
                            mm = pe.matmul(bank[:, t * P:(t + 1) * P], grid_t[:, 4 * h + t, :], w(W_QO),
                                           start=True, stop=True)
                        mm.then_inc(done, 1)
                if name == "ht":
                    bank, done = fill(pe, it, part, "ht")
                    pe.wait_ge(gelu_ready.sem, gelu_ready.at(run, b + 1))
                    pe.transpose(bank[:, 0:P], feat_b[:, :, :].rearrange("p t f -> p (t f)"), ident).then_inc(done, 1)
                if name == "of":
                    bank, done = fill(pe, it, part, "of")
                    was_read(pe, it, part, "ht")
                    pe.matmul(bank[:, 0:P], hid_t[:, :], w(W_O2), start=True, stop=True).then_inc(done, 1)

            def sample(it, n):
                pe.wait_ge(weighted.sem, weighted.at(it, n + 1))
                g = gathered[:, n % RING, :].rearrange("p (k n) -> p k n", k=HEADS)
                for h in range(2):
                    pe.wait_ge(points_copied.sem, points_copied.at(it, 2 * n + h - 1))
                    for k in range(4):
                        mm = pe.transpose(points_ps[:, h, k * P:(k + 1) * P], g[:, 4 * h + k, 0:2 * C], ident)
                    mm.then_inc(points_full.sem, 1)

            def project(it, n):
                pe.wait_ge(values_used.sem, values_used.at(it, n - 1))
                for h in range(2):
                    pe.wait_ge(points_copied.sem, points_copied.at(it, 2 * n + h + 1))
                    for k in range(4):
                        mm = pe.matmul(kv_ps[:, 2 * (n % 2) + h, k * P:(k + 1) * P],
                                       sampled_t[:, n % 2, 4 * h + k, :], w(W_KV), start=True, stop=True)
                    mm.then_inc(kv_full.sem, 1)

            def part1(it, names):
                run, name = it, names[0]
                for h in range(2):
                    if name == f"in{h}":
                        if isinstance(it, int) and it == 0:
                            pe.wait_ge(cls_loaded.sem, 16)
                        else:
                            pe.wait_ge(attended_ready.sem, attended_ready.at(it - 1, TILES + 4 * h + 4))
                        bank, done = fill(pe, it, 1, f"in{h}")
                        for t in range(4):
                            mm = pe.transpose(bank[:, t * P:(t + 1) * P],
                                              attended[:, 4 * h + t, :, :].rearrange("p b c -> p (b c)"), ident)
                        mm.then_inc(done, 1)
                    if name == f"cena{h}":
                        was_read(pe, it, 1, f"in{h}")
                        product(it, 1, f"cena{h}", c_sb[:, C_CENTER, :], h0[:, cols(h)])
                    if name == f"vara{h}":
                        was_read(pe, it, 1, f"cena{h}")
                        product(it, 1, f"vara{h}", c_sb[:, C_MEAN, :], rs1[:, cols(h)])
                    if name == f"k{h}":
                        pe.wait_ge(mix_in_ready.sem, mix_in_ready.at(run, h + 1))
                        for key, m in (("k", W_K), ("v", W_V), ("r", W_R)):
                            product(it, 1, f"{key}{h}", w(m), hn[:, cols(h)])
                    if name == "wo0":
                        pe.wait_ge(mixed_ready.sem, mixed_ready.at(run, 1))
                        product(it, 1, f"wo{h}", w(W_O), wide[:, 0, cols(h)])
                    if name == "cenf0":
                        was_read(pe, it, 1, f"wo{h}")
                        product(it, 1, f"cenf{h}", c_sb[:, C_CENTER, :], x1[:, cols(h)])
                    if name == "varf0":
                        was_read(pe, it, 1, f"cenf{h}")
                        product(it, 1, f"varf{h}", c_sb[:, C_MEAN, :], rs1[:, cols(h)])
                    if name.startswith(f"up{h}"):
                        pe.wait_ge(ffn_in_ready.sem, ffn_in_ready.at(run, h + 1))
                        for use in names:
                            product(it, 1, use, w(W_UP + int(use[-1])), hn[:, cols(h)])
                    if name == "gate0":
                        product(it, 1, f"gate{h}", w(W_FR), hn[:, cols(h)])
                    if name == f"dn{h}":
                        bank, done = fill(pe, it, 1, f"dn{h}")
                        pe.wait_ge(hidden_ready.sem, hidden_ready.at(run, 4 * h + 4))
                        for k in range(4):
                            mm = pe.matmul(bank, w(W_DN + k), hidden[:, 4 * h + k, :], start=(k == 0), stop=(k == 3))
                        mm.then_inc(done, 1)

            def part2(it, names):
                run, name = it - 1, names[0]
                for h in range(2):
                    if name == "cenm0":
                        pe.wait_ge(hm_ready.sem, hm_ready.at(run, h + 1))
                        product(it, 2, f"cenm{h}", c_sb[:, C_CENTER, :], hm[:, cols(h)])
                    if name == "varm0":
                        was_read(pe, it, 2, f"cenm{h}")
                        product(it, 2, f"varm{h}", c_sb[:, C_MEAN, :], rm[:, cols(h)])
                    if name == "route0":
                        bank, done = fill(pe, it, 2, f"route{h}")
                        pe.wait_ge(nm_ready.sem, nm_ready.at(run, h + 1))
                        for t in range(4):
                            mm = pe.matmul(bank[:, t * P:(t + 1) * P], nm[:, (4 * h + t) * P:(4 * h + t + 1) * P],
                                           w(W_RT), start=True, stop=True)
                        mm.then_inc(done, 1)
                    if name == "one0":
                        bank, done = fill(pe, it, 2, f"one{h}")
                        pe.wait_ge(choice_ready.sem, choice_ready.at(run, 1))
                        for t in range(4):
                            mm = pe.transpose(bank[:, t * P:(t + 1) * P], choice[:, 4 * h + t, :], ident)
                        mm.then_inc(done, 1)
                    if name.startswith(f"mu{h}"):
                        was_read(pe, it, 2, f"one{h}")
                        for use in names:
                            k = int(use[-1])
                            bank, done = fill(pe, it, 2, use)
                            pe.matmul(bank, w(W_MU + k), nm[:, cols(h)], start=True, stop=False)
                            pe.matmul(bank, sel_sb[:, k, :], others_t[:, cols(h)], start=False,
                                      stop=True).then_inc(done, 1)
                    if name == f"md{h}":
                        bank, done = fill(pe, it, 2, f"md{h}")
                        was_read(pe, it, 2, f"mu{h}.6")
                        was_read(pe, it, 2, f"mu{h}.7")
                        pe.matmul(bank, w(W_B2), choice_t[:, cols(h)], start=True, stop=False)
                        for k in range(2 * BLOCKS):
                            mm = pe.matmul(bank, w(W_MD + k), moe_hidden[:, k, :], start=False,
                                           stop=(k == 2 * BLOCKS - 1))
                        mm.then_inc(done, 1)
                    if name == f"out{h}":
                        bank, done = fill(pe, it, 2, f"out{h}")
                        was_read(pe, it, 2, f"md{h}")
                        for t in range(4):
                            mm = pe.transpose(bank[:, t * P:(t + 1) * P],
                                              xm[:, (4 * h + t) * P:(4 * h + t + 1) * P], ident)
                        mm.then_inc(done, 1)

            def iteration(it):
                for j in range(3 * PAIR_TILES):
                    if samples_in(it) and j % 3 == 0:
                        sample(it, j // 3)
                    if samples_in(it) and j % 3 == 1:
                        project(it, j // 3)
                    for part, names in stages(it, j):
                        if part == 1:
                            part1(it, names)
                        elif part == 2:
                            part2(it, names)
                        else:
                            prepare(it, part, names[0])

            for _, part, names in SCHEDULE:
                if part in ("q0", "q1"):
                    prepare(-1, part, names[0])
            all_iterations(pe, iteration)

        @block.scalar
        def _(act):
            def mark(ins):
                return scalar_steps.mark(ins)

            def after(n):
                act.wait_ge(scalar_steps.sem, scalar_steps.value(n))

            act.wait_ge(loaded.sem, 16 * 5)
            act.activation(sel_sb[:, :, :], sel_stage, ACT.Copy).then_inc(sel_cast.sem, 1)
            act.wait_ge(bias_full.sem, 1)
            mark(act.activation(fold[:, 0:2], work_ps[:, 0, 0:2], ACT.Copy))
            mark(act.activation(fold[:, 2:4], work_ps[:, 0, 2:4], ACT.Copy, scale=-1.0))
            n = mark(act.activation(fold[:, 4:6], work_ps[:, 0, 4:6], ACT.Copy))
            after(n)
            act.sem_inc(bias_read.sem, 1)
            act.wait_ge(filled.sem, 1)

            def prepare(it, part, name):
                b, run = int(part[1]), it + 1
                if name == "qt0":
                    for h in range(2):
                        bank, done = full(act, it, part, f"qt{h}")
                        act.activation(grid_t[:, 4 * h:4 * h + 4, :].rearrange("p t n -> p (t n)"), bank,
                                       ACT.Copy).then_inc(done, 1)
                if name == "qo0":
                    for h in range(2):
                        bank, done = full(act, it, part, f"qo{h}")
                        act.activation(qo_tmp[:, 4 * h:4 * h + 4, :],
                                       bank.rearrange("p (t n) -> p t n", t=4)[:, :, 0:C + OFF],
                                       ACT.Copy).then_inc(done, 1)
                if name == "ht":
                    bank, done = full(act, it, part, "ht")
                    act.activation(hid_t[:, :], bank[:, 0:P], ACT.Copy).then_inc(done, 1)

            def inverse_std(it, b):
                run = it + 1
                act.wait_ge(feature_var.sem, feature_var.at(run, b + 1))
                n = mark(act.activation(feat_r[:, 0, :], feat_s[:, 1, :], ACT.Ln, scale=1.0 / OFF, bias=eps_col))
                after(n)
                act.activation(feat_r[:, 1, :], feat_r[:, 0, :], ACT.Exp, scale=-0.5).then_inc(feature_std.sem, 1)

            def gelu_exponential(it, b):
                run = it + 1
                act.wait_ge(gelu_arg.sem, gelu_arg.at(run, b + 1))
                act.activation(feat_c[:, :, :], feat_a[:, :, :], ACT.Exp,
                               scale=-2.0 * (2.0 / np.pi) ** 0.5).then_inc(gelu_exp.sem, 1)

            def commit_queries(it, b):
                act.wait_ge(scores_ready.sem, scores_ready.at(it - 1, TILES * (b + 1)))
                act.activation(queries[:, b, :, :], qo_tmp[:, :, 0:C], ACT.Copy).then_inc(queries_ready.sem, 1)

            def copy_points(it, n):
                for h in range(2):
                    act.wait_ge(points_full.sem, points_full.at(it, 2 * n + h + 1))
                    act.wait_ge(kv_full.sem, kv_full.at(it, 2 * (n - 2) + h + 1))
                    act.activation(sampled_t[:, n % 2, 4 * h:4 * h + 4, :].rearrange("p k n -> p (k n)"),
                                   points_ps[:, h, :], ACT.Copy).then_inc(points_copied.sem, 1)

            def exponentials(it, n):
                act.wait_ge(scores_ready.sem, scores_ready.at(it, n + 1))
                act.activation(probs[:, n % 2, :, :], shifted[:, :, :], ACT.Exp,
                               scale=DH ** -0.5).then_inc(probs_ready.sem, 1)

            def centered(it, part, name, h, x, squares):
                bank, done = full(act, it, part, name)
                act.activation(x[:, cols(h)], bank, ACT.Copy)
                act.activation(squares[:, cols(h)], bank, ACT.Square).then_inc(done, 1)

            def inverse_stds(it, part, name, h, std, ready):
                bank, done = full(act, it, part, name)
                act.activation(std[:, cols(h)], bank, ACT.Ln, bias=eps_col).then_inc(done, 1)
                was_read(act, it, part, name)
                act.activation(std[:, cols(h)], std[:, cols(h)], ACT.Exp, scale=-0.5).then_inc(ready, 1)

            def part1(it, names):
                run, name = it, names[0]
                for h in range(2):
                    if name == f"in{h}":
                        bank, done = full(act, it, 1, f"in{h}")
                        act.wait_ge(hm_ready.sem, hm_ready.at(run, 0))
                        act.activation(h0[:, cols(h)], bank, ACT.Copy).then_inc(done, 1)
                    if name == f"cena{h}":
                        act.wait_ge(ffn_in_ready.sem, ffn_in_ready.at(run, 0))
                        centered(it, 1, f"cena{h}", h, xc, rs1)
                    if name == f"vara{h}":
                        bank, done = full(act, it, 1, f"vara{h}")
                        n = mark(act.activation(rs1[:, cols(h)], bank, ACT.Ln, bias=eps_col))
                        act.activation(rs2[:, cols(h)], bank, ACT.Ln, scale=1.0 + EPS,
                                       bias=eps2_col).then_inc(done, 1)
                        after(n)
                        mark(act.activation(rs1[:, cols(h)], rs1[:, cols(h)], ACT.Exp, scale=-0.5))
                        was_read(act, it, 1, f"vara{h}")
                        act.activation(rs2[:, cols(h)], rs2[:, cols(h)], ACT.Exp, scale=-0.5).then_inc(stds_a.sem, 1)
                    if name == f"k{h}":
                        for key, to, n, func, scale in (("k", xc, 0, ACT.Identity, 1.0),
                                                        ("v", rs1, 1, ACT.Identity, 1.0),
                                                        ("r", rs2, 2, ACT.Exp, -1.0)):
                            bank, done = full(act, it, 1, f"{key}{h}")
                            act.activation(to[:, cols(h)], bank, func, bias=fold[:, n:n + 1],
                                           scale=scale).then_inc(done, 1)
                    if name == "cenf0":
                        centered(it, 1, f"cenf{h}", h, xc, rs1)
                    if name == "varf0":
                        inverse_stds(it, 1, f"varf{h}", h, rs1, stds_f.sem)
                    if name.startswith(f"up{h}"):
                        for use in names:
                            k = int(use[-1])
                            bank, done = full(act, it, 1, use)
                            act.activation(hidden[:, 4 * h + k, :], bank, ACT.Relu,
                                           bias=fold[:, 4 + k % 2:5 + k % 2]).then_inc(done, 1)
                        for use in names:
                            k = int(use[-1])
                            was_read(act, it, 1, use)
                            act.activation(hidden[:, 4 * h + k, :], hidden[:, 4 * h + k, :],
                                           ACT.Square).then_inc(hidden_ready.sem, 1)
                    if name == "gate0":
                        bank, done = full(act, it, 1, f"gate{h}")
                        act.activation(rs2[:, cols(h)], bank, ACT.Exp, bias=fold[:, 3:4],
                                       scale=-1.0).then_inc(done, 1)

            def update_exponentials(it):
                act.wait_ge(diff_ready.sem, diff_ready.at(it, 1))
                n = mark(act.activation(wide[:, 2, :], hn[:, :], ACT.Relu, bias=decay[:, 3:4]))
                m = mark(act.activation(wide[:, 3, :], hn[:, :], ACT.Relu, bias=decay[:, 2:3], scale=-1.0))
                after(n)
                mark(act.activation(wide[:, 2, :], wide[:, 2, :], ACT.Exp, scale=-1.0))
                after(m)
                act.activation(wide[:, 3, :], wide[:, 3, :], ACT.Exp, scale=-1.0).then_inc(update_gates.sem, 1)

            def output_exponentials(it):
                n = mark(act.activation(wide[:, 0, :], hn[:, :], ACT.Relu))
                m = mark(act.activation(wide[:, 1, :], hn[:, :], ACT.Relu, scale=-1.0))
                after(n)
                mark(act.activation(wide[:, 0, :], wide[:, 0, :], ACT.Exp, scale=-1.0))
                after(m)
                act.activation(wide[:, 1, :], wide[:, 1, :], ACT.Exp, scale=-1.0).then_inc(output_gates.sem, 1)

            def part2(it, names):
                run, name = it - 1, names[0]
                for h in range(2):
                    if name == "cenm0":
                        act.wait_ge(written.sem, written.at(run, 0))
                        centered(it, 2, f"cenm{h}", h, xm, rm)
                    if name == "varm0":
                        inverse_stds(it, 2, f"varm{h}", h, rm, stds_m.sem)
                    if name == "one0":
                        bank, done = full(act, it, 2, f"one{h}")
                        act.activation(choice_t[:, cols(h)], bank, ACT.Copy)
                        act.activation(others_t[:, cols(h)], bank, ACT.Identity, bias=minus1_col).then_inc(done, 1)
                    if name.startswith(f"mu{h}"):
                        for use in names:
                            k = int(use[-1])
                            bank, done = full(act, it, 2, use)
                            at = V_MB1 + k % BLOCKS
                            act.activation(moe_hidden[:, k, :], bank, ACT.Relu,
                                           bias=v_sb[:, at:at + 1]).then_inc(done, 1)
                    if name == f"out{h}":
                        bank, done = full(act, it, 2, f"out{h}")
                        act.activation(rm[:, cols(h)], bank, ACT.Copy).then_inc(done, 1)

            def iteration(it):
                parts = parts_of(it)
                for j in range(3 * PAIR_TILES):
                    n = j // 3
                    if samples_in(it) and j % 3 == 0:
                        copy_points(it, n)
                    for part, names in stages(it, j):
                        if part == 1:
                            part1(it, names)
                        elif part == 2:
                            part2(it, names)
                        else:
                            prepare(it, part, names[0])
                    for b in range(2):
                        if f"q{b}" in parts:
                            if j == SCALAR_AT[f"feature_std{b}"]:
                                inverse_std(it, b)
                            if j == SCALAR_AT[f"gelu_exp{b}"]:
                                gelu_exponential(it, b)
                    if "q0" in parts and j == COMMIT_AT[0]:
                        commit_queries(it + 1, 0)
                    if samples_in(it) and j == COMMIT_AT[1]:
                        commit_queries(it, 1)
                    if 1 in parts and j == SCALAR_AT["update"]:
                        update_exponentials(it)
                    if 1 in parts and j == SCALAR_AT["output"]:
                        output_exponentials(it)
                    if j % 3 == 2:
                        if n >= 1 and samples_in(it):
                            exponentials(it, n - 1)
                        elif n == 0 and 1 in parts and not (isinstance(it, int) and it == 0):
                            exponentials(it - 1, PAIR_TILES - 1)

            for b in range(2):
                for _, part, names in SCHEDULE:
                    if part == f"q{b}":
                        prepare(-1, part, names[0])
                        if names[0] == "qo0":
                            inverse_std(-1, b)
                            gelu_exponential(-1, b)
                if b == 0:
                    commit_queries(0, 0)
            all_iterations(act, iteration, scalar_steps)

        @block.vector
        def _(dve):
            def mark(ins):
                return vector_steps.mark(ins)

            def after(n):
                dve.wait_ge(vector_steps.sem, vector_steps.value(n))

            def step(ins):
                after(mark(ins))

            def rows(at, n, shape):
                return v_sb[:, at:at + n].unsqueeze(1).broadcast_to(shape)

            mark(dve.memset(eps_col, EPS))
            mark(dve.memset(eps2_col, EPS * EPS))
            mark(dve.memset(minus1_col, -1.0))
            mark(dve.memset(image_base[:, :], 0.0))
            mark(dve.memset(choice[:, :, :], 0.0))
            mark(dve.memset(state_o[:, 0:1], -1e38))
            mark(dve.memset(state_p[:, 0:1], 0.0))
            mark(dve.memset(state_q[:, 0:1], 0.0))
            dve.wait_ge(loaded.sem, 16 * 5)
            step(dve.tensor_scalar(decay[:, 0:1], v_sb[:, V_W:V_W + 1], 1.0 / SEQ, None, ALU.mult))
            step(dve.tensor_scalar(decay[:, 1:2], v_sb[:, V_U:V_U + 1], 1.0 / SEQ, None, ALU.mult))
            step(dve.tensor_tensor(decay[:, 2:3], decay[:, 0:1], decay[:, 1:2], ALU.add))
            step(dve.tensor_scalar(decay[:, 3:4], decay[:, 2:3], -1.0, None, ALU.mult))
            dve.wait_ge(bias_read.sem, 1)
            step(dve.tensor_scalar(w_sb[:, W_K:W_R + 1, :], w_sb[:, W_K:W_R + 1, :], v_sb[:, V_G1:V_G1 + 1],
                                   None, ALU.mult))
            step(dve.tensor_scalar(w_sb[:, W_UP:W_UP + 4, :], w_sb[:, W_UP:W_UP + 4, :],
                                   v_sb[:, V_G2:V_G2 + 1], None, ALU.mult))
            dve.tensor_scalar(w_sb[:, W_FR, :], w_sb[:, W_FR, :], v_sb[:, V_G2:V_G2 + 1],
                              None, ALU.mult).then_inc(folded.sem, 1)
            dve.wait_ge(folded.sem, 1)
            dve.sem_inc(filled.sem, 1)

            def grid_corners(it, b):
                dve.wait_ge(grid_loaded.sem, grid_loaded.at(it + 1, 16 * (b + 1)))
                px = grid_px[:, :, :].rearrange("p t (k c) -> p (t k) c", c=C)
                wt = s_sb[:, S_GW:S_GW + 4 * TILES].unsqueeze(2).broadcast_to([P, 4 * TILES, C])
                step(dve.tensor_tensor(px, px, wt, ALU.mult))
                px = grid_px[:, :, :]
                dve.tensor_tensor(px[:, :, 0:2 * C], px[:, :, 0:2 * C], px[:, :, 2 * C:4 * C], ALU.add).then_inc(grid_summed.sem, 1)

            def features(it, b):
                part, shape = f"q{b}", [P, TILES, OFF]
                was_read(dve, it, part, "qo0")
                was_read(dve, it, part, "qo1")
                step(dve.tensor_tensor(feat_a[:, :, :], qo_tmp[:, :, C:C + OFF], rows(V_BO1, OFF, shape), ALU.add))
                step(dve.tensor_reduce(feat_s[:, 0, :], feat_a[:, :, :], AX_X, ALU.add))
                step(dve.tensor_scalar(feat_s[:, 0, :], feat_s[:, 0, :], 1.0 / OFF, None, ALU.mult))
                step(dve.tensor_tensor(feat_a[:, :, :], feat_a[:, :, :],
                                       feat_s[:, 0, :].unsqueeze(2).broadcast_to(shape), ALU.subtract))
                step(dve.tensor_tensor(feat_b[:, :, :], feat_a[:, :, :], feat_a[:, :, :], ALU.mult))
                dve.tensor_reduce(feat_s[:, 1, :], feat_b[:, :, :], AX_X, ALU.add).then_inc(feature_var.sem, 1)

            def normalised(it, b):
                shape = [P, TILES, OFF]
                dve.wait_ge(feature_std.sem, feature_std.at(it + 1, b + 1))
                step(dve.tensor_tensor(feat_b[:, :, :], feat_a[:, :, :],
                                       feat_r[:, 1, :].unsqueeze(2).broadcast_to(shape), ALU.mult))
                step(dve.tensor_tensor(feat_b[:, :, :], feat_b[:, :, :], rows(V_LNG, OFF, shape), ALU.mult))
                step(dve.tensor_tensor(feat_b[:, :, :], feat_b[:, :, :], rows(V_LNB, OFF, shape), ALU.add))
                step(dve.tensor_tensor(feat_a[:, :, :], feat_b[:, :, :], feat_b[:, :, :], ALU.mult))
                step(dve.tensor_scalar(feat_a[:, :, :], feat_a[:, :, :], 0.044715, 1.0, ALU.mult, ALU.add))
                dve.tensor_tensor(feat_a[:, :, :], feat_a[:, :, :], feat_b[:, :, :], ALU.mult).then_inc(gelu_arg.sem, 1)

            def gelu(it, b):
                dve.wait_ge(gelu_exp.sem, gelu_exp.at(it + 1, b + 1))
                step(dve.tensor_scalar(feat_c[:, :, :], feat_c[:, :, :], 1.0, None, ALU.add))
                step(dve.reciprocal(feat_c[:, :, :], feat_c[:, :, :]))
                dve.tensor_tensor(feat_b[:, :, :], feat_b[:, :, :], feat_c[:, :, :], ALU.mult).then_inc(gelu_ready.sem, 1)

            def sampling_points(it, b):
                bank, done = full(dve, it, f"q{b}", "of")
                off = bank[:, 0:P].rearrange("p (t f) -> p t f", t=TILES)
                dve.tensor_tensor(feat_a[:, :, :], off, rows(V_BO2, OFF, [P, TILES, OFF]), ALU.add).then_inc(done, 1)
                was_read(dve, it, f"q{b}", "of")
                base = s_sb[:, S_BASE:S_BASE + P]
                step(dve.scalar_tensor_tensor(
                    frac[:, :, :, :].rearrange("p t h x -> p (t h x)"),
                    feat_a[:, :, :].rearrange("p t f -> p (t f)"), 4.0, base, ALU.mult, ALU.add))
                step(dve.tensor_scalar(frac[:, :, :, :], frac[:, :, :, :], 0.0, SIDE - 1.0, ALU.max, ALU.min))
                step(dve.tensor_scalar(corner[:, :, :, :], frac[:, :, :, :], -0.5, 0.0, ALU.add, ALU.max))
                step(dve.tensor_scalar(corner[:, :, :, :], corner[:, :, :, :], ROUND, None, ALU.add))
                step(dve.tensor_scalar(corner[:, :, :, :], corner[:, :, :, :], -ROUND, SIDE - 2.0, ALU.add, ALU.min))
                step(dve.tensor_tensor(frac[:, :, :, :], frac[:, :, :, :], corner[:, :, :, :], ALU.subtract))

            def commit_points(it, b):
                away = feat_c[:, :, :].rearrange("p t (h x) -> p t h x", x=2)
                flat = feat_a[:, :, 0:HEADS]
                a = mark(dve.tensor_scalar(away, frac[:, :, :, :], -1.0, 1.0, ALU.mult, ALU.add))
                n = mark(dve.scalar_tensor_tensor(flat, corner[:, :, :, 0], float(SIDE), corner[:, :, :, 1],
                                                  ALU.mult, ALU.add))
                after(n)
                dve.tensor_scalar(index[:, b, :].rearrange("p (t h) -> p t h", t=TILES), flat,
                                  image_base[:, 0:1], None, ALU.add).then_inc(index_ready.sem, 1)
                for x in range(2):
                    for y in range(2):
                        wx = (away, frac[:, :, :, :])[x][:, :, :, 0]
                        wy = (away, frac[:, :, :, :])[y][:, :, :, 1]
                        n = mark(dve.tensor_tensor(mix[:, b, :, :, 2 * y + x], wx, wy, ALU.mult))
                dve.wait_ge(index_ready.sem, index_ready.at(it, b + 1))
                step(dve.tensor_scalar(image_base[:, :], image_base[:, :], float(IMAGE_ROWS), None, ALU.add))

            def weigh(it, n):
                b, t, s = n // TILES, n % TILES, n % RING
                dve.wait_ge(slot_gathered[s].sem, slot_gathered[s].at(it, (n // RING + 1) * HEADS * 16))
                g = gathered[:, s, :].rearrange("p (k c) -> p k c", c=C)
                wt = mix[:, b, t, :, :].rearrange("p h k -> p (h k)").unsqueeze(2).broadcast_to([P, 4 * HEADS, C])
                step(dve.tensor_tensor(g, g, wt, ALU.mult))
                g = gathered[:, s, :].rearrange("p (k n) -> p k n", k=HEADS)
                dve.tensor_tensor(g[:, :, 0:2 * C], g[:, :, 0:2 * C], g[:, :, 2 * C:4 * C], ALU.add).then_inc(weighted.sem, 1)

            def kv(n):
                return kv_ps[:, 2 * (n % 2):2 * (n % 2) + 2, :].rearrange("p a (k n) -> p (a k) n", k=4)

            def score(it, n):
                b, t = n // TILES, n % TILES
                dve.wait_ge(kv_full.sem, kv_full.at(it, 2 * n + 2))
                dve.wait_ge(queries_ready.sem, queries_ready.at(it, b + 1))
                step(dve.tensor_tensor(qk[:, :, :], kv(n)[:, :, 0:C],
                                       queries[:, b, t, :].unsqueeze(1).broadcast_to([P, HEADS, C]), ALU.mult))
                step(dve.tensor_reduce(scores[:, :, :], qk[:, :, :].rearrange("p k (h d) -> p k h d", h=HEADS),
                                       AX_X, ALU.add))
                step(dve.tensor_reduce(top[:, :], scores[:, :, :].rearrange("p k h -> p h k"), AX_X, ALU.max))
                dve.tensor_tensor(shifted[:, :, :], scores[:, :, :],
                                  top[:, :].unsqueeze(1).broadcast_to([P, HEADS, HEADS]),
                                  ALU.subtract).then_inc(scores_ready.sem, 1)

            def attend(it, n):
                b, t = n // TILES, n % TILES
                e = probs[:, n % 2, :, :]
                dve.wait_ge(probs_ready.sem, probs_ready.at(it, n + 1))
                dve.tensor_tensor(av[:, :, :].rearrange("p k (h d) -> p k h d", h=HEADS),
                                  kv(n)[:, :, C:2 * C].rearrange("p k (h d) -> p k h d", h=HEADS),
                                  e.unsqueeze(3).broadcast_to([P, HEADS, HEADS, DH]), ALU.mult).then_inc(values_used.sem, 1)
                m = mark(dve.tensor_reduce(prob_sum[:, :], e.rearrange("p k h -> p h k"), AX_X, ALU.add))
                dve.wait_ge(values_used.sem, values_used.at(it, n + 1))
                a = mark(dve.tensor_reduce(attended_raw[:, :], av[:, :, :].rearrange("p k c -> p c k"), AX_X, ALU.add))
                after(m)
                step(dve.reciprocal(prob_sum[:, :], prob_sum[:, :]))
                if t % 4 == 0 and b == 0:
                    was_read(dve, *attended_taken(it, t))
                dve.tensor_tensor(attended[:, t, b, :].rearrange("p (h d) -> p h d", h=HEADS),
                                  attended_raw[:, :].rearrange("p (h d) -> p h d", h=HEADS),
                                  prob_sum[:, :].unsqueeze(2).broadcast_to([P, HEADS, DH]),
                                  ALU.mult).then_inc(attended_ready.sem, 1)

            def attended_taken(it, t):
                return it, 1, f"in{t // 4}"

            def mix_input(it, h):
                dve.wait_ge(stds_a.sem, stds_a.at(it, h + 1))
                mark(dve.tensor_tensor(x1[:, cols(h)], xc[:, cols(h)], rs1[:, cols(h)], ALU.mult))
                dve.tensor_tensor(hn[:, cols(h)], xc[:, cols(h)], rs2[:, cols(h)], ALU.mult).then_inc(mix_in_ready.sem, 1)

            def running_max(it):
                for key in ("k0", "v0", "r0", "k1", "v1", "r1"):
                    was_read(dve, it, 1, key)
                step(dve.tensor_tensor_scan(state_o[:, 1:NQ + 1], decay[:, 0:1].broadcast_to([P, NQ]), xc[:, :],
                                            state_o[:, 0:1], ALU.add, ALU.max))
                dve.scalar_tensor_tensor(hn[:, :], xc[:, :], decay[:, 1:2], state_o[:, 0:NQ],
                                         ALU.add, ALU.subtract).then_inc(diff_ready.sem, 1)

            def running_sums(it):
                dve.wait_ge(diff_ready.sem, diff_ready.at(it, 1))
                dve.wait_ge(update_gates.sem, update_gates.at(it, 1))
                n = mark(dve.tensor_tensor(xc[:, :], wide[:, 3, :], rs1[:, :], ALU.mult))
                mark(dve.tensor_tensor_scan(state_q[:, 1:NQ + 1], wide[:, 2, :], wide[:, 3, :],
                                            state_q[:, 0:1], ALU.mult, ALU.add))
                after(n)
                step(dve.tensor_tensor_scan(state_p[:, 1:NQ + 1], wide[:, 2, :], xc[:, :],
                                            state_p[:, 0:1], ALU.mult, ALU.add))

            def mixed_sums(it):
                dve.wait_ge(output_gates.sem, output_gates.at(it, 1))
                a = mark(dve.tensor_tensor(hn[:, :], wide[:, 0, :], state_q[:, 0:NQ], ALU.mult))
                b = mark(dve.tensor_tensor(rs1[:, :], wide[:, 1, :], rs1[:, :], ALU.mult))
                c = mark(dve.tensor_tensor(wide[:, 0, :], wide[:, 0, :], state_p[:, 0:NQ], ALU.mult))
                after(a)
                d = mark(dve.tensor_tensor(hn[:, :], hn[:, :], wide[:, 1, :], ALU.add))
                after(c)
                step(dve.tensor_tensor(wide[:, 0, :], wide[:, 0, :], rs1[:, :], ALU.add))

            def mixed(it):
                step(dve.scalar_tensor_tensor(hn[:, :], rs2[:, :], 1.0, hn[:, :], ALU.add, ALU.mult))
                step(dve.reciprocal(hn[:, :], hn[:, :]))
                dve.tensor_tensor(wide[:, 0, :], wide[:, 0, :], hn[:, :], ALU.mult).then_inc(mixed_ready.sem, 1)
                if isinstance(it, int) and it == 0:
                    for state in (state_o, state_p, state_q):
                        step(dve.tensor_copy(state[:, 0:1], state[:, 1:2]))

            def add_mix(it):
                for h in range(2):
                    bank, done = full(dve, it, 1, f"wo{h}")
                    dve.tensor_tensor(x1[:, cols(h)], x1[:, cols(h)], bank, ALU.add).then_inc(done, 1)

            def ffn_input(it):
                for h in range(2):
                    dve.wait_ge(stds_f.sem, stds_f.at(it, h + 1))
                    dve.tensor_tensor(hn[:, cols(h)], xc[:, cols(h)], rs1[:, cols(h)],
                                      ALU.mult).then_inc(ffn_in_ready.sem, 1)

            def gate(it):
                for h in range(2):
                    was_read(dve, it, 1, f"gate{h}")
                step(dve.tensor_scalar(rs2[:, :], rs2[:, :], 1.0, None, ALU.add))
                step(dve.reciprocal(rs2[:, :], rs2[:, :]))

            def add_ffn(it, h):
                bank, done = full(dve, it, 1, f"dn{h}")
                dve.tensor_tensor(rs2[:, cols(h)], bank, rs2[:, cols(h)], ALU.mult).then_inc(done, 1)
                was_read(dve, it, 1, f"dn{h}")
                step(dve.tensor_tensor(x1[:, cols(h)], x1[:, cols(h)], rs2[:, cols(h)], ALU.add))
                dve.tensor_tensor(hm[:, cols(h)], h0[:, cols(h)], x1[:, cols(h)], ALU.add).then_inc(hm_ready.sem, 1)

            def moe_input(it):
                for h in range(2):
                    dve.wait_ge(stds_m.sem, stds_m.at(it - 1, h + 1))
                    dve.tensor_tensor(nm[:, cols(h)], xm[:, cols(h)], rm[:, cols(h)],
                                      ALU.mult).then_inc(nm_ready.sem, 1)

            def take_logits(it):
                for h in range(2):
                    bank, done = full(dve, it, 2, f"route{h}")
                    dve.tensor_tensor(
                        logits[:, 4 * h:4 * h + 4, :, :],
                        bank.rearrange("p (t b e) -> p t b e", t=4, b=4)[:, :, 0:2, :],
                        v_sb[:, V_RB:V_RB + EXPERTS].unsqueeze(1).unsqueeze(1).broadcast_to([P, 4, 2, EXPERTS]),
                        ALU.add).then_inc(done, 1)

            def choose(it):
                shape = [P, 2 * TILES, EXPERTS]
                flat = logits[:, :, :, :].rearrange("p t b e -> p (t b) e")
                most = logit_top[:, :, :].rearrange("p t b -> p (t b)")
                ranks = s_sb[:, S_RANK:S_RANK + EXPERTS].unsqueeze(1).broadcast_to(shape)
                for h in range(2):
                    was_read(dve, it, 2, f"route{h}")
                step(dve.tensor_reduce(most, flat, AX_X, ALU.max))
                step(dve.tensor_tensor(flat, flat, most.unsqueeze(2).broadcast_to(shape), ALU.is_equal))
                step(dve.tensor_tensor(flat, flat, ranks, ALU.mult))
                step(dve.tensor_reduce(most, flat, AX_X, ALU.max))
                dve.tensor_tensor(choice[:, :, 0:2 * EXPERTS].rearrange("p t (b e) -> p t b e", b=2),
                                  logits[:, :, :, :],
                                  logit_top[:, :, :].unsqueeze(3).broadcast_to([P, TILES, 2, EXPERTS]),
                                  ALU.is_equal).then_inc(choice_ready.sem, 1)

            def add_moe(it, h):
                bank, done = full(dve, it, 2, f"md{h}")
                dve.scalar_tensor_tensor(xm[:, cols(h)], bank, 0.0, hm[:, cols(h)], ALU.max, ALU.add).then_inc(done, 1)

            def iteration(it):
                parts = parts_of(it)
                first = isinstance(it, int) and it == 0
                for j in range(3 * PAIR_TILES):
                    n = j // 3
                    if samples_in(it) and j % 3 == 0:
                        weigh(it, n)
                    if j % 3 == 1:
                        if n >= 2 and samples_in(it):
                            attend(it, n - 2)
                        elif n < 2 and 1 in parts and not first:
                            attend(it - 1, PAIR_TILES + n - 2)
                    if j % 3 == 2:
                        if n >= 1 and samples_in(it):
                            score(it, n - 1)
                        elif n == 0 and 1 in parts and not first:
                            score(it - 1, PAIR_TILES - 1)
                    for b in range(2):
                        if f"q{b}" in parts:
                            for name, stage in (("grid_corners", grid_corners), ("features", features),
                                                ("normalised", normalised), ("gelu", gelu),
                                                ("sampling_points", sampling_points)):
                                if j == VECTOR_AT[f"{name}{b}"]:
                                    stage(it, b)
                    if "q0" in parts and j == COMMIT_AT[0]:
                        commit_points(it + 1, 0)
                    if samples_in(it) and j == COMMIT_AT[1]:
                        commit_points(it, 1)
                    if 1 in parts:
                        for h in range(2):
                            if j == VECTOR_AT[f"mix_input{h}"]:
                                mix_input(it, h)
                            if j == VECTOR_AT[f"add_ffn{h}"]:
                                add_ffn(it, h)
                        if j == VECTOR_AT["running_max"]:
                            running_max(it)
                        if j == VECTOR_AT["running_sums"]:
                            running_sums(it)
                        if j == VECTOR_AT["mixed_sums"]:
                            mixed_sums(it)
                        if j == VECTOR_AT["mixed"]:
                            mixed(it)
                        if j == VECTOR_AT["add_mix"]:
                            add_mix(it)
                        if j == VECTOR_AT["ffn_input"]:
                            ffn_input(it)
                        if j == VECTOR_AT["gate"]:
                            gate(it)
                    if 2 in parts:
                        if j == VECTOR_AT["moe_input"]:
                            moe_input(it)
                        if j == VECTOR_AT["take_logits"]:
                            take_logits(it)
                        if j == VECTOR_AT["choose"]:
                            choose(it)
                        for h in range(2):
                            if j == VECTOR_AT[f"add_moe{h}"]:
                                add_moe(it, h)

            for b in range(2):
                grid_corners(-1, b)
                features(-1, b)
                normalised(-1, b)
                gelu(-1, b)
                sampling_points(-1, b)
                if b == 0:
                    commit_points(0, 0)
            all_iterations(dve, iteration, vector_steps)


def _padded(blocks, rows=P, cols=P):
    m = np.zeros((rows, cols), np.float32)
    for r, c, a in blocks:
        m[r:r + a.shape[0], c:c + a.shape[1]] = a
    return m


def _weight_matrices(i):
    wq, wk, wv = i["L0_tok_W_q"].T, i["L0_tok_W_k"].T, i["L0_tok_W_v"].T
    twice = lambda a: _padded([(0, 0, a), (a.shape[0], a.shape[1], a)])
    ms = [None] * N_WEIGHTS
    ms[W_KV] = _padded([(r, c, a) for r in (0, C) for c, a in ((0, wk), (C, wv))])
    ms[W_QO] = _padded([(r, c, a) for r in (0, C) for c, a in ((0, wq), (C, i["L0_tok_W_o1"]))])
    ms[W_O2] = _padded([(OFF * t, OFF * t, i["L0_tok_W_o2"]) for t in range(TILES)])
    for m, name in ((W_K, "Wk"), (W_V, "Wv"), (W_R, "Wr"), (W_O, "Wo"), (W_FR, "Wr_ffn")):
        ms[m] = twice(i["L0_attn_" + name])
    ms[W_RT] = twice(i["L0_ffn_router_w"].T)
    ms[W_B2] = twice(i["L0_ffn_b2"])
    up = i["L0_ffn_W1"].transpose(1, 0, 2).reshape(C, EXPERTS * EH)
    down = i["L0_ffn_W2"].reshape(EXPERTS * EH, C)
    for b in range(2):
        for m in range(2):
            part = slice(m * P, (m + 1) * P)
            ms[W_UP + 2 * b + m] = _padded([(b * C, 0, i["L0_attn_Wk_ffn"][:, part])])
            ms[W_DN + 2 * b + m] = _padded([(0, b * C, i["L0_attn_Wv_ffn"][part])])
        for m in range(BLOCKS):
            part = slice(m * P, (m + 1) * P)
            ms[W_MU + BLOCKS * b + m] = _padded([(b * C, 0, up[:, part])])
            ms[W_MD + BLOCKS * b + m] = _padded([(0, b * C, down[part])])
    return np.ascontiguousarray(np.stack(ms, axis=1))


def _vectors(i):
    m = np.zeros((P, N_VECTORS), np.float32)
    for at, name in ((V_G1, "g1"), (V_B1, "b1"), (V_G2, "g2"), (V_B2, "b2"), (V_U, "spatial_first"),
                     (V_W, "spatial_decay")):
        m[0:C, at] = m[C:2 * C, at] = i["L0_attn_" + name]
    m[:, V_MB1:V_MB1 + BLOCKS] = i["L0_ffn_b1"].reshape(BLOCKS, P).T
    for at, name in ((V_BO1, "L0_tok_b_o1"), (V_LNG, "L0_tok_ln_g"), (V_LNB, "L0_tok_ln_b"),
                     (V_BO2, "L0_tok_b_o2"), (V_RB, "L0_ffn_router_b")):
        m[:, at:at + i[name].shape[0]] = i[name]
    return m


def _consts():
    m = np.zeros((P, N_CONSTS, P), np.float32)
    eye = np.eye(P, dtype=np.float32)
    mean = _padded([(r, r, np.full((C, C), 1.0 / C, np.float32)) for r in (0, C)])
    m[:, C_IDENT], m[:, C_CENTER], m[:, C_MEAN] = eye, eye - mean, mean
    for b in range(2):
        for k in range(BLOCKS):
            for e in range(EXPERTS // BLOCKS):
                row = EXPERTS * b + EXPERTS // BLOCKS * k + e
                m[row, C_SEL + BLOCKS * b + k, EH * e:EH * (e + 1)] = MASKED
    return m


def _grid_positions():
    x = (np.linspace(-1.0, 1.0, GRID).astype(np.float32) + 1.0) * 0.5 * (SIDE - 1)
    x0 = np.clip(np.floor(x), 0, SIDE - 2)
    return x.astype(np.float32), x0.astype(np.int64), np.clip(x - x0, 0.0, 1.0).astype(np.float32)


def _shape_vectors():
    x, _, w = _grid_positions()
    q = np.arange(NQ)
    gy, gx = q // GRID, q % GRID
    wx = np.stack([1 - w[gx], w[gx]], 1)
    wy = np.stack([1 - w[gy], w[gy]], 1)
    corners = (wy[:, :, None] * wx[:, None, :]).reshape(TILES, P, 4)
    base = np.tile(np.stack([x[gx], x[gy]], 1), HEADS).reshape(TILES, P, 2 * HEADS)
    m = np.zeros((P, N_SHAPE_VECTORS), np.float32)
    m[:, S_GW:S_GW + 4 * TILES] = corners.transpose(1, 0, 2).reshape(P, -1)
    m[:, S_BASE:S_RANK] = base.transpose(1, 0, 2).reshape(P, -1)
    m[:, S_RANK:] = EXPERTS - np.arange(EXPERTS)
    return m


def kernel(**inputs):
    import concourse.bacc as _bacc
    from concourse.bass_utils import run_bass_kernel_spmd as _run

    i = {name: np.asarray(a) for name, a in inputs.items()}
    x = i["x"]
    images = x.shape[0]
    last = x.transpose(0, 3, 2, 1)
    paired = np.empty((images, SIDE - 1, SIDE, 2, C), x.dtype)
    paired[:, :, :, 0] = last[:, :-1]
    paired[:, :, :, 1] = last[:, 1:]
    _, x0, _ = _grid_positions()
    grid = paired[:, x0][:, :, x0[:, None] + np.arange(2)].transpose(0, 2, 1, 3, 4, 5)
    grid = grid.reshape(images, TILES, P, PATCH).transpose(0, 2, 1, 3).reshape(images, P, TILES * PATCH)
    arrays = {
        "pixels": paired.reshape(images * IMAGE_ROWS, 2 * C),
        "grid": np.ascontiguousarray(grid),
        "cls": np.ascontiguousarray(np.broadcast_to(i["cls_tok"].reshape(1, C), (P, C))),
        "weights": _weight_matrices(i),
        "vectors": _vectors(i),
        "consts": _consts(),
        "shape_vectors": _shape_vectors(),
    }
    nc = _bacc.Bacc("TRN2", target_bir_lowering=False, num_devices=1)
    args = [nc.dram_tensor(n, a.shape, mybir.dt.from_np(a.dtype), kind="ExternalInput").ap()
            for n, a in arrays.items()]
    out = nc.dram_tensor("out", (images, SEQ, C), F32, kind="ExternalOutput").ap()
    vit_kernel(nc, *args, out)
    return _run(nc, [arrays], core_ids=[0]).results[0]["out"]
```

```python
from contextlib import ExitStack

import numpy as np

import concourse.bass as bass
from concourse import mybir

ALU = mybir.AluOpType
ACT = mybir.ActivationFunctionType
AX_X = mybir.AxisListType.X
F32 = mybir.dt.float32
BF16 = mybir.dt.bfloat16
I32 = mybir.dt.int32

P = 128
C = 64
SIDE = 128
GRID = 32
NQ = GRID * GRID
TILES = NQ // P
HEADS = 8
DH = C // HEADS
OFF = 16
PATCH = 4 * C
PAIR_TILES = 2 * TILES
SEQ = NQ + 1
HALF = NQ // 2
HID = 4 * C
EXPERTS = 32
EH = 16
BLOCKS = EXPERTS * EH // P
IMAGE_ROWS = (SIDE - 1) * SIDE
RING = 4
MASKED = 3.0e38
EPS = 1e-5

W_KV, W_QO, W_O2, W_K, W_V, W_R, W_O, W_FR, W_RT, W_B2 = range(10)
W_UP, W_DN, W_MU, W_MD = 10, 14, 18, 26
N_WEIGHTS = 34
C_IDENT, C_CENTER, C_MEAN, C_SEL = 0, 1, 2, 3
N_CONSTS = 3 + 2 * BLOCKS

V_G1, V_B1, V_G2, V_B2, V_U, V_W, V_MB1 = 0, 1, 2, 3, 4, 5, 6
V_BO1 = 10
V_LNG, V_LNB, V_BO2, V_RB = V_BO1 + OFF, V_BO1 + 2 * OFF, V_BO1 + 3 * OFF, V_BO1 + 4 * OFF
N_VECTORS = V_RB + EXPERTS
S_GW, S_BASE, S_RANK = 0, TILES * 4, TILES * (4 + 2 * HEADS)
N_SHAPE_VECTORS = S_RANK + EXPERTS

SLOTS = 4 * (2 * TILES) // 2

SCHEDULE = [
    (0, 2, ["cenm0", "cenm1"]), (1, 2, ["varm0", "varm1"]), (1, 1, ["in0"]), (2, 1, ["cena0"]), (2, 1, ["vara0"]),
    (3, 1, ["in1"]), (4, 2, ["route0", "route1"]), (4, 1, ["k0", "v0", "r0"]), (4, 1, ["cena1"]), (6, 1, ["vara1"]),
    (6, 2, ["one0", "one1"]), (7, "q0", ["qt0", "qt1"]), (7, "q0", ["qo0", "qo1"]), (7, 1, ["k1", "v1", "r1"]),
    (8, 2, ["mu0.0", "mu0.1"]), (9, 2, ["mu0.2", "mu0.3"]), (10, 2, ["mu0.4", "mu0.5"]),
    (10, 2, ["mu0.6", "mu0.7"]), (11, 2, ["md0"]), (12, 2, ["mu1.0"]), (12, 2, ["mu1.1", "mu1.2"]),
    (13, "q0", ["ht"]), (14, 2, ["out0"]), (14, 2, ["mu1.3", "mu1.4"]), (14, "q0", ["of"]), (15, 2, ["mu1.5"]),
    (17, 2, ["mu1.6", "mu1.7"]), (17, 1, ["wo0", "wo1"]), (17, 2, ["md1"]), (19, 1, ["cenf0", "cenf1"]),
    (19, "q1", ["qt0", "qt1"]), (19, 1, ["varf0", "varf1"]), (19, "q1", ["qo0", "qo1"]), (20, 2, ["out1"]),
    (22, 1, ["gate0", "gate1"]), (23, 1, ["up0.0", "up0.1"]), (23, 1, ["up0.2", "up0.3"]),
    (25, 1, ["up1.0", "up1.1"]), (26, 1, ["up1.2", "up1.3"]), (26, 1, ["dn0"]), (28, "q1", ["ht"]),
    (29, 1, ["dn1"]), (30, "q1", ["of"]),
]
VECTOR_AT = {
    "moe_input": 2, "mix_input0": 4, "take_logits": 5, "choose": 6, "mix_input1": 7, "grid_corners0": 7,
    "features0": 8, "running_max": 9, "running_sums": 10, "normalised0": 11, "add_moe0": 13, "gelu0": 13,
    "mixed_sums": 14, "mixed_exponent": 15, "mixed": 16, "sampling_points0": 16, "add_mix": 17, "add_moe1": 19,
    "grid_corners1": 19, "ffn_input": 22, "features1": 22, "gate_exponent": 26, "normalised1": 26,
    "add_ffn0": 28, "gelu1": 28, "add_ffn1": 31, "sampling_points1": 31,
}
SCALAR_AT = {
    "update": 8, "feature_std0": 8, "gelu_exp0": 10, "output": 11, "mixed_log": 14, "mixed_quotient": 15,
    "feature_std1": 22, "gelu_exp1": 25, "gate": 26,
}
COMMIT_AT = (18, 0)
ROUND = float(2 ** 23)


def work_uses(parts):
    names = [(part, name) for _, part, group in SCHEDULE if part in parts for name in group]
    return {key: n for n, key in enumerate(names)}, len(names)


class Signal:

    def __init__(self, sem, per):
        self.sem, self.per = sem, per

    def at(self, run, n):
        value = run * self.per + n
        return max(value, 0) if isinstance(run, int) else value


class Steps:

    def __init__(self, sem, per_loop):
        self.sem, self.per, self.count, self.loop = sem, per_loop, 0, None

    def mark(self, ins):
        ins.then_inc(self.sem, 1)
        self.count += 1
        return self.count

    def value(self, n):
        return n if self.loop is None else n + self.loop * self.per

    def enter(self, turn):
        self.loop, self.start = turn, self.count

    def leave(self, turns):
        assert self.count - self.start == self.per, (self.count - self.start, self.per)
        self.loop, self.count = None, self.start + turns * self.per


def vit_kernel(nc, pixels, grid, cls, weights, vectors, consts, shape_vectors, out):
    images = out.shape[0]
    pairs = images // 2
    first_looped, last_looped = 2, pairs - 2
    VECTOR_STEPS, SCALAR_STEPS = 133, 18

    all_parts = (1, 2, "q0", "q1")
    position, per_iteration = {}, {}
    for parts in (("q0", "q1"), (1, "q0", "q1"), all_parts, (1, 2), (2,)):
        position[parts], per_iteration[parts] = work_uses(parts)

    def parts_of(it):
        if not isinstance(it, int):
            return all_parts
        if it < 0:
            return ("q0", "q1")
        parts = ((1,) if it <= pairs else ()) + ((2,) if it > 0 else ())
        return parts + (("q0", "q1") if it < pairs - 1 else ())

    def uses_before(it):
        if not isinstance(it, int):
            return (it - first_looped) * per_iteration[all_parts] + uses_before(first_looped)
        return sum(per_iteration[parts_of(x)] for x in range(-1, it))

    def bank_of(it, part, name):
        n = position[parts_of(it)][(part, name)]
        if isinstance(it, int):
            n += uses_before(it)
            return n % 2, n // 2
        before = (it - first_looped) * (per_iteration[all_parts] // 2) + uses_before(first_looped) // 2
        return n % 2, before + n // 2

    with ExitStack() as ctx:
        def sb(name, shape, dt=F32):
            return ctx.enter_context(nc.sbuf_tensor(name, shape, dt))

        def signal(name, per=1):
            return Signal(ctx.enter_context(nc.semaphore(name)), per)

        w_sb = sb("w_sb", [P, N_WEIGHTS, P])
        c_sb = sb("c_sb", [P, 3, P])
        sel_sb = sb("sel_sb", [P, 2 * BLOCKS, P], BF16)
        v_sb = sb("v_sb", [P, N_VECTORS])
        s_sb = sb("s_sb", [P, N_SHAPE_VECTORS])
        small = sb("small", [P, 4])
        eps_col, eps2_col, minus1_col, one_col = (small[:, k:k + 1] for k in range(4))
        fold = sb("fold", [P, 8])
        decay = sb("decay", [P, 4])
        image_base = sb("image_base", [P, 1])
        gathered = sb("gathered", [P, RING, HEADS * PATCH])
        sampled_t = sb("sampled_t", [P, 2, HEADS, P])
        products = sb("products", [P, 2, HEADS, C])
        scores = sb("scores", [P, 2, HEADS, HEADS])
        shifted = sb("shifted", [P, 2, HEADS, HEADS])
        top = sb("top", [P, 2, HEADS])
        probs = sb("probs", [P, 2, HEADS, HEADS])
        prob_sum = sb("prob_sum", [P, 2, HEADS])
        attended_raw = sb("attended_raw", [P, 2, C])
        attended = sb("attended", [P, TILES, 2, C])
        grid_px = sb("grid_px", [P, TILES, PATCH])
        grid_t = sb("grid_t", [P, TILES, P])
        qo_tmp = sb("qo_tmp", [P, TILES, C + OFF])
        feat_a = sb("feat_a", [P, TILES, OFF])
        feat_b = sb("feat_b", [P, TILES, OFF])
        feat_c = sb("feat_c", [P, TILES, OFF])
        feat_s = sb("feat_s", [P, 2, TILES])
        feat_r = sb("feat_r", [P, 2, TILES])
        hid_t = sb("hid_t", [P, P])
        frac = sb("frac", [P, TILES, HEADS, 2])
        corner = sb("corner", [P, TILES, HEADS, 2])
        queries = sb("queries", [P, 2, TILES, C])
        mix = sb("mix", [P, 2, TILES, HEADS, 4])
        index = sb("index", [P, 2, TILES * HEADS], I32)
        h0 = sb("h0", [P, NQ])
        xc = sb("xc", [P, NQ])
        rs1 = sb("rs1", [P, NQ])
        rs2 = sb("rs2", [P, NQ])
        relu_r = sb("relu_r", [P, NQ])
        x1 = sb("x1", [P, NQ])
        hn = sb("hn", [P, NQ])
        state_o = sb("state_o", [P, NQ + 1])
        state_p = sb("state_p", [P, NQ + 1])
        state_q = sb("state_q", [P, NQ + 1])
        wide = sb("wide", [P, 4, NQ])
        hidden = wide[:, :, :].rearrange("p a (h n) -> p (a h) n", h=2)
        hm = sb("hm", [P, NQ])
        xm = sb("xm", [P, NQ])
        rm = sb("rm", [P, NQ])
        nm = sb("nm", [P, NQ])
        logits = sb("logits", [P, TILES, 2, EXPERTS])
        logit_top = sb("logit_top", [P, TILES, 2])
        choice = sb("choice", [P, TILES, P])
        choice_t = sb("choice_t", [P, NQ])
        others_t = sb("others_t", [P, NQ], BF16)
        moe_hidden = sb("moe_hidden", [P, 2 * BLOCKS, HALF])
        sel_stage = moe_hidden[:, 0:2, :].rearrange("p a (s n) -> p (a s) n", n=P)

        points_ps = ctx.enter_context(nc.psum_tensor("points_ps", [P, 2, 512], F32))
        kv_ps = ctx.enter_context(nc.psum_tensor("kv_ps", [P, 4, 512], F32))
        work_ps = ctx.enter_context(nc.psum_tensor("work_ps", [P, 2, 512], F32))

        loaded = signal("loaded")
        cls_loaded = signal("cls_loaded")
        sel_cast = signal("sel_cast")
        filled = signal("filled")
        bias_full = signal("bias_full")
        bias_read = signal("bias_read")
        folded = signal("folded")
        slot_gathered = [signal(f"slot_gathered{k}", PAIR_TILES // RING * HEADS * 16) for k in range(RING)]
        tiles_started = signal("tiles_started", PAIR_TILES)
        weighted = signal("weighted", PAIR_TILES)
        points_full = signal("points_full", 2 * PAIR_TILES)
        points_copied = signal("points_copied", 2 * PAIR_TILES)
        kv_full = signal("kv_full", 2 * PAIR_TILES)
        scores_ready = signal("scores_ready", TILES)
        probs_ready = signal("probs_ready", TILES)
        values_used = signal("values_used", TILES)
        attended_ready = signal("attended_ready", TILES)
        grid_requested = signal("grid_requested", 2)
        halves_done = signal("halves_done", 2)
        grid_loaded = signal("grid_loaded", 32)
        grid_summed = signal("grid_summed", 2)
        feature_var = signal("feature_var", 2)
        feature_std = signal("feature_std", 2)
        gelu_arg = signal("gelu_arg", 2)
        gelu_exp = signal("gelu_exp", 2)
        gelu_ready = signal("gelu_ready", 2)
        index_ready = signal("index_ready", 2)
        queries_ready = signal("queries_ready", 2)
        bank_full = [signal(f"bank_full{k}") for k in range(2)]
        bank_read = [signal(f"bank_read{k}") for k in range(2)]
        stds_a = signal("stds_a", 2)
        mix_in_ready = signal("mix_in_ready", 2)
        diff_ready = signal("diff_ready")
        update_gates = signal("update_gates")
        output_gates = signal("output_gates")
        quotient_log_arg = signal("quotient_log_arg")
        quotient_log = signal("quotient_log")
        quotient_exp_arg = signal("quotient_exp_arg")
        quotient = signal("quotient")
        mixed_ready = signal("mixed_ready")
        gate_r_ready = signal("gate_r_ready", 2)
        gate_log = signal("gate_log", 2)
        gate_exp_arg = signal("gate_exp_arg")
        gate_ready = signal("gate_ready")
        stds_f = signal("stds_f", 2)
        ffn_in_ready = signal("ffn_in_ready", 2)
        hidden_ready = signal("hidden_ready", 8)
        hm_ready = signal("hm_ready", 2)
        stds_m = signal("stds_m", 2)
        nm_ready = signal("nm_ready", 2)
        choice_ready = signal("choice_ready")
        written = signal("written", 32)
        vector_steps = Steps(ctx.enter_context(nc.semaphore("vector_steps")), VECTOR_STEPS)
        scalar_steps = Steps(ctx.enter_context(nc.semaphore("scalar_steps")), SCALAR_STEPS)

        ident = c_sb[:, C_IDENT, :]
        block = ctx.enter_context(nc.Block())

        def cols(h):
            return slice(h * HALF, (h + 1) * HALF)

        def fill(eng, it, part, name, *inputs):
            k, before = bank_of(it, part, name)
            eng.wait_ge(bank_read[k].sem, before)
            others = [key for key in inputs if bank_of(it, part, key)[0] != k]
            if others:
                was_read(eng, it, part, max(others, key=lambda key: position[parts_of(it)][(part, key)]))
            return work_ps[:, k, :], bank_full[k].sem

        def full(eng, it, part, name):
            k, before = bank_of(it, part, name)
            eng.wait_ge(bank_full[k].sem, before + 1)
            return work_ps[:, k, :], bank_read[k].sem

        def was_read(eng, it, part, name):
            k, before = bank_of(it, part, name)
            eng.wait_ge(bank_read[k].sem, before + 1)

        def all_iterations(eng, iteration, steps=None):
            for it in range(min(first_looped, pairs)):
                iteration(it)
            if last_looped >= first_looped:
                with eng.Fori(first_looped, last_looped + 1) as it:
                    if steps:
                        steps.enter(it - first_looped)
                    iteration(it)
                if steps:
                    steps.leave(last_looped + 1 - first_looped)
            for it in range(max(last_looped + 1, first_looped), pairs + 2):
                iteration(it)

        def samples_in(it):
            return not isinstance(it, int) or it < pairs

        def stages(it, j):
            return [(part, names) for slot, part, names in SCHEDULE if slot == j and part in parts_of(it)]

        @block.sync
        def _(sp):
            sp.dma_start(w_sb[:, :, :], weights).then_inc(loaded.sem, 16)
            sp.dma_start(v_sb[:, :], vectors).then_inc(loaded.sem, 16)
            sp.dma_start(c_sb[:, :, :], consts[:, 0:3, :]).then_inc(loaded.sem, 16)
            sp.dma_start(sel_stage, consts[:, C_SEL:N_CONSTS, :]).then_inc(loaded.sem, 16)
            sp.dma_start(s_sb[:, :], shape_vectors).then_inc(loaded.sem, 16)

            def load_grid(it, b):
                if b == 1:
                    was_read(sp, it, "q0", "qt1")
                elif not isinstance(it, int) or it >= 0:
                    was_read(sp, it - 1, "q1", "qt1")
                sp.sem_inc(grid_requested.sem, 1)
                sp.dma_start(grid_px[:, :, :].rearrange("p t n -> p (t n)"),
                             grid[2 * (it + 1) + b, :, :]).then_inc(grid_loaded.sem, 16)

            def store(it):
                for h in range(2):
                    was_read(sp, it, 2, f"out{h}")
                    sp.sem_inc(halves_done.sem, 1)
                if isinstance(it, int) and it == 1:
                    for b in range(2):
                        to = out[b * (images // 2):(b + 1) * (images // 2), 0:1, :].rearrange("b o c -> o b c")
                        sp.dma_start(to, rm[0:1, 0:C].unsqueeze(1).broadcast_to([1, images // 2, C])).then_inc(written.sem, 16)
                else:
                    for b in range(2):
                        to = out[2 * (it - 2) + b, 1:SEQ, :].rearrange("(t p) c -> p t c", p=P)
                        sp.dma_start(to, rm[:, :].rearrange("p (t b c) -> p t b c", t=TILES, b=2)[:, :, b, :]
                                     ).then_inc(written.sem, 16)

            def iteration(it):
                parts = parts_of(it)
                for b in range(2):
                    if "q0" in parts:
                        load_grid(it, b)
                if 2 in parts:
                    store(it)

            load_grid(-1, 0)
            sp.dma_start(attended[:, :, :, :].rearrange("p t b c -> p (t b) c"),
                         cls.unsqueeze(1).broadcast_to([P, 2 * TILES, C])).then_inc(cls_loaded.sem, 16)
            load_grid(-1, 1)
            all_iterations(sp, iteration)
            sp.wait_ge(written.sem, written.at(pairs, 32))

        @block.gpsimd
        def _(pool):
            def iteration(it):
                if not samples_in(it):
                    return
                for n in range(PAIR_TILES):
                    if n % TILES == 0:
                        pool.wait_ge(index_ready.sem, index_ready.at(it, n // TILES + 1))
                    pool.wait_ge(points_full.sem, points_full.at(it, 2 * (n - RING) + 2))
                    pool.sem_inc(tiles_started.sem, 1)
                    for k in range(HEADS):
                        at = (n % TILES) * HEADS + k
                        pool.indirect_dma_start(
                            gathered[:, n % RING, k * PATCH:(k + 1) * PATCH], None, pixels,
                            bass.IndirectOffsetOnAxis(ap=index[:, n // TILES, at:at + 1], axis=0),
                        ).then_inc(slot_gathered[n % RING].sem, 16)

            all_iterations(pool, iteration)

        @block.tensor
        def _(pe):
            def w(n):
                return w_sb[:, n, :]

            def product(it, part, name, lhsT, rhs, *inputs):
                bank, filled_now = fill(pe, it, part, name, *inputs)
                pe.matmul(bank, lhsT, rhs, start=True, stop=True).then_inc(filled_now, 1)

            pe.wait_ge(loaded.sem, 16 * 5)
            for n, (m, shift) in enumerate([(W_K, V_B1), (W_V, V_B1), (W_R, V_B1), (W_FR, V_B2),
                                            (W_UP, V_B2), (W_UP + 1, V_B2),
                                            (W_UP + 2, V_B2), (W_UP + 3, V_B2)]):
                mm = pe.matmul(work_ps[:, 0, n:n + 1], w(m), v_sb[:, shift:shift + 1], start=True, stop=True)
            mm.then_inc(bias_full.sem, 1)
            pe.wait_ge(bias_read.sem, 1)
            pe.wait_ge(folded.sem, 1)
            pe.wait_ge(sel_cast.sem, 1)
            pe.wait_ge(filled.sem, 1)

            def prepare(it, part, name):
                b, run = int(part[1]), it + 1
                if name == "qt0":
                    pe.wait_ge(grid_summed.sem, grid_summed.at(run, b + 1))
                    for h in range(2):
                        bank, done = fill(pe, it, part, f"qt{h}")
                        for t in range(4):
                            mm = pe.transpose(bank[:, t * P:(t + 1) * P], grid_px[:, 4 * h + t, 0:2 * C], ident)
                        mm.then_inc(done, 1)
                if name == "qo0":
                    for h in range(2):
                        bank, done = fill(pe, it, part, f"qo{h}", f"qt{h}")
                        for t in range(4):
                            mm = pe.matmul(bank[:, t * P:(t + 1) * P], grid_t[:, 4 * h + t, :], w(W_QO),
                                           start=True, stop=True)
                        mm.then_inc(done, 1)
                if name == "ht":
                    bank, done = fill(pe, it, part, "ht")
                    pe.wait_ge(gelu_ready.sem, gelu_ready.at(run, b + 1))
                    pe.transpose(bank[:, 0:P], feat_b[:, :, :].rearrange("p t f -> p (t f)"), ident).then_inc(done, 1)
                if name == "of":
                    bank, done = fill(pe, it, part, "of", "ht")
                    pe.matmul(bank[:, 0:P], hid_t[:, :], w(W_O2), start=True, stop=True).then_inc(done, 1)

            def sample(it, n):
                pe.wait_ge(weighted.sem, weighted.at(it, n + 1))
                g = gathered[:, n % RING, :].rearrange("p (k n) -> p k n", k=HEADS)
                for h in range(2):
                    pe.wait_ge(points_copied.sem, points_copied.at(it, 2 * n + h - 1))
                    for k in range(4):
                        mm = pe.transpose(points_ps[:, h, k * P:(k + 1) * P], g[:, 4 * h + k, 0:2 * C], ident)
                    mm.then_inc(points_full.sem, 1)

            def project(it, m):
                pe.wait_ge(values_used.sem, values_used.at(it, m))
                for n in (2 * m, 2 * m + 1):
                    for h in range(2):
                        pe.wait_ge(points_copied.sem, points_copied.at(it, 2 * n + h + 1))
                        for k in range(4):
                            mm = pe.matmul(kv_ps[:, 2 * (n % 2) + h, k * P:(k + 1) * P],
                                           sampled_t[:, n % 2, 4 * h + k, :], w(W_KV), start=True, stop=True)
                        mm.then_inc(kv_full.sem, 1)

            def part1(it, names):
                run, name = it, names[0]
                for h in range(2):
                    if name == f"in{h}":
                        if isinstance(it, int) and it == 0:
                            pe.wait_ge(cls_loaded.sem, 16)
                        else:
                            pe.wait_ge(attended_ready.sem, attended_ready.at(it - 1, TILES // 2 + 2 * h + 2))
                        bank, done = fill(pe, it, 1, f"in{h}")
                        for t in range(4):
                            mm = pe.transpose(bank[:, t * P:(t + 1) * P],
                                              attended[:, 4 * h + t, :, :].rearrange("p b c -> p (b c)"), ident)
                        mm.then_inc(done, 1)
                    if name == f"cena{h}":
                        product(it, 1, f"cena{h}", c_sb[:, C_CENTER, :], h0[:, cols(h)],
                                f"in{h}")
                    if name == f"vara{h}":
                        product(it, 1, f"vara{h}", c_sb[:, C_MEAN, :], rs1[:, cols(h)],
                                f"cena{h}")
                    if name == f"k{h}":
                        pe.wait_ge(mix_in_ready.sem, mix_in_ready.at(run, h + 1))
                        for key, m in (("k", W_K), ("v", W_V), ("r", W_R)):
                            product(it, 1, f"{key}{h}", w(m), hn[:, cols(h)])
                    if name == "wo0":
                        pe.wait_ge(mixed_ready.sem, mixed_ready.at(run, 1))
                        product(it, 1, f"wo{h}", w(W_O), wide[:, 0, cols(h)])
                    if name == "cenf0":
                        product(it, 1, f"cenf{h}", c_sb[:, C_CENTER, :], x1[:, cols(h)],
                                f"wo{h}")
                    if name == "varf0":
                        product(it, 1, f"varf{h}", c_sb[:, C_MEAN, :], rs1[:, cols(h)],
                                f"cenf{h}")
                    if name.startswith(f"up{h}"):
                        for use in names:
                            product(it, 1, use, w(W_UP + int(use[-1])), hn[:, cols(h)])
                    if name == "gate0":
                        pe.wait_ge(ffn_in_ready.sem, ffn_in_ready.at(run, h + 1))
                        product(it, 1, f"gate{h}", w(W_FR), hn[:, cols(h)])
                    if name == f"dn{h}":
                        bank, done = fill(pe, it, 1, f"dn{h}")
                        pe.wait_ge(hidden_ready.sem, hidden_ready.at(run, 4 * h + 4))
                        for k in range(4):
                            mm = pe.matmul(bank, w(W_DN + k), hidden[:, 4 * h + k, :], start=(k == 0), stop=(k == 3))
                        mm.then_inc(done, 1)

            def part2(it, names):
                run, name = it - 1, names[0]
                for h in range(2):
                    if name == "cenm0":
                        pe.wait_ge(hm_ready.sem, hm_ready.at(run, h + 1))
                        product(it, 2, f"cenm{h}", c_sb[:, C_CENTER, :], hm[:, cols(h)])
                    if name == "varm0":
                        product(it, 2, f"varm{h}", c_sb[:, C_MEAN, :], rm[:, cols(h)],
                                f"cenm{h}")
                    if name == "route0":
                        bank, done = fill(pe, it, 2, f"route{h}")
                        pe.wait_ge(nm_ready.sem, nm_ready.at(run, h + 1))
                        for t in range(4):
                            mm = pe.matmul(bank[:, t * P:(t + 1) * P], nm[:, (4 * h + t) * P:(4 * h + t + 1) * P],
                                           w(W_RT), start=True, stop=True)
                        mm.then_inc(done, 1)
                    if name == "one0":
                        bank, done = fill(pe, it, 2, f"one{h}")
                        pe.wait_ge(choice_ready.sem, choice_ready.at(run, 1))
                        for t in range(4):
                            mm = pe.transpose(bank[:, t * P:(t + 1) * P], choice[:, 4 * h + t, :], ident)
                        mm.then_inc(done, 1)
                    if name.startswith(f"mu{h}"):
                        for use in names:
                            k = int(use[-1])
                            bank, done = fill(pe, it, 2, use, f"one{h}")
                            pe.matmul(bank, w(W_MU + k), nm[:, cols(h)], start=True, stop=False)
                            pe.matmul(bank, sel_sb[:, k, :], others_t[:, cols(h)], start=False,
                                      stop=True).then_inc(done, 1)
                    if name == f"md{h}":
                        bank, done = fill(pe, it, 2, f"md{h}", f"mu{h}.6", f"mu{h}.7")
                        pe.matmul(bank, w(W_B2), choice_t[:, cols(h)], start=True, stop=False)
                        for k in range(2 * BLOCKS):
                            mm = pe.matmul(bank, w(W_MD + k), moe_hidden[:, k, :], start=False,
                                           stop=(k == 2 * BLOCKS - 1))
                        mm.then_inc(done, 1)
                    if name == f"out{h}":
                        bank, done = fill(pe, it, 2, f"out{h}", f"md{h}")
                        for t in range(4):
                            mm = pe.transpose(bank[:, t * P:(t + 1) * P],
                                              xm[:, (4 * h + t) * P:(4 * h + t + 1) * P], ident)
                        mm.then_inc(done, 1)

            def iteration(it):
                for j in range(SLOTS):
                    if samples_in(it) and j % 2 == 0:
                        sample(it, j // 2)
                    if samples_in(it) and j % 4 == 3:
                        project(it, j // 4)
                    for part, names in stages(it, j):
                        if part == 1:
                            part1(it, names)
                        elif part == 2:
                            part2(it, names)
                        else:
                            prepare(it, part, names[0])

            for _, part, names in SCHEDULE:
                if part in ("q0", "q1"):
                    prepare(-1, part, names[0])
            all_iterations(pe, iteration)

        @block.scalar
        def _(act):
            def mark(ins):
                return scalar_steps.mark(ins)

            def after(n):
                act.wait_ge(scalar_steps.sem, scalar_steps.value(n))

            act.preload_act_table_set("natural_log_exp_and_others")
            act.wait_ge(loaded.sem, 16 * 5)
            act.activation(sel_sb[:, :, :], sel_stage, ACT.Copy).then_inc(sel_cast.sem, 1)
            act.wait_ge(bias_full.sem, 1)
            mark(act.activation(fold[:, 0:2], work_ps[:, 0, 0:2], ACT.Copy))
            mark(act.activation(fold[:, 2:4], work_ps[:, 0, 2:4], ACT.Copy, scale=-1.0))
            n = mark(act.activation(fold[:, 4:6], work_ps[:, 0, 4:6], ACT.Copy))
            after(n)
            act.sem_inc(bias_read.sem, 1)
            act.wait_ge(filled.sem, 1)

            def prepare(it, part, name):
                b, run = int(part[1]), it + 1
                if name == "qt0":
                    for h in range(2):
                        bank, done = full(act, it, part, f"qt{h}")
                        act.activation(grid_t[:, 4 * h:4 * h + 4, :].rearrange("p t n -> p (t n)"), bank,
                                       ACT.Copy).then_inc(done, 1)
                if name == "qo0":
                    for h in range(2):
                        bank, done = full(act, it, part, f"qo{h}")
                        act.activation(qo_tmp[:, 4 * h:4 * h + 4, :],
                                       bank.rearrange("p (t n) -> p t n", t=4)[:, :, 0:C + OFF],
                                       ACT.Copy).then_inc(done, 1)
                if name == "ht":
                    bank, done = full(act, it, part, "ht")
                    act.activation(hid_t[:, :], bank[:, 0:P], ACT.Copy).then_inc(done, 1)

            def inverse_std(it, b):
                run = it + 1
                act.wait_ge(feature_var.sem, feature_var.at(run, b + 1))
                n = mark(act.activation(feat_r[:, 0, :], feat_s[:, 1, :], ACT.Ln, scale=1.0 / OFF, bias=eps_col))
                after(n)
                act.activation(feat_r[:, 1, :], feat_r[:, 0, :], ACT.Exp, scale=-0.5).then_inc(feature_std.sem, 1)

            def gelu_exponential(it, b):
                run = it + 1
                act.wait_ge(gelu_arg.sem, gelu_arg.at(run, b + 1))
                act.activation(feat_c[:, :, :], feat_a[:, :, :], ACT.Exp,
                               scale=-2.0 * (2.0 / np.pi) ** 0.5).then_inc(gelu_exp.sem, 1)

            def commit_queries(it, b):
                act.wait_ge(scores_ready.sem, scores_ready.at(it - 1, TILES // 2 * (b + 1)))
                act.activation(queries[:, b, :, :], qo_tmp[:, :, 0:C], ACT.Copy).then_inc(queries_ready.sem, 1)

            def copy_points(it, n):
                for h in range(2):
                    act.wait_ge(points_full.sem, points_full.at(it, 2 * n + h + 1))
                    act.wait_ge(kv_full.sem, kv_full.at(it, 2 * (n - 2) + h + 1))
                    act.activation(sampled_t[:, n % 2, 4 * h:4 * h + 4, :].rearrange("p k n -> p (k n)"),
                                   points_ps[:, h, :], ACT.Copy).then_inc(points_copied.sem, 1)

            def exponentials(it, m):
                act.wait_ge(scores_ready.sem, scores_ready.at(it, m + 1))
                act.activation(probs[:, :, :, :], shifted[:, :, :, :], ACT.Exp,
                               scale=DH ** -0.5).then_inc(probs_ready.sem, 1)

            def gate_parts(it, key, h, n, shrink, grow):
                bank, done = full(act, it, 1, f"{key}{h}")
                a = mark(act.activation(shrink[:, cols(h)], bank, ACT.Abs, bias=fold[:, n:n + 1], scale=-1.0))
                act.activation(grow[:, cols(h)], bank, ACT.Relu, bias=fold[:, n:n + 1], scale=-1.0).then_inc(done, 1)
                after(a)
                return act.activation(shrink[:, cols(h)], shrink[:, cols(h)], ACT.Exp, scale=-1.0)

            def centered(it, part, name, h, x, squares):
                bank, done = full(act, it, part, name)
                act.activation(x[:, cols(h)], bank, ACT.Copy)
                act.activation(squares[:, cols(h)], bank, ACT.Square).then_inc(done, 1)

            def inverse_stds(it, part, name, h, std, ready):
                bank, done = full(act, it, part, name)
                act.activation(std[:, cols(h)], bank, ACT.Ln, bias=eps_col).then_inc(done, 1)
                was_read(act, it, part, name)
                act.activation(std[:, cols(h)], std[:, cols(h)], ACT.Exp, scale=-0.5).then_inc(ready, 1)

            def part1(it, names):
                run, name = it, names[0]
                for h in range(2):
                    if name == f"in{h}":
                        bank, done = full(act, it, 1, f"in{h}")
                        act.wait_ge(hm_ready.sem, hm_ready.at(run, 0))
                        act.activation(h0[:, cols(h)], bank, ACT.Copy).then_inc(done, 1)
                    if name == f"cena{h}":
                        act.wait_ge(ffn_in_ready.sem, ffn_in_ready.at(run, 0))
                        centered(it, 1, f"cena{h}", h, xc, rs1)
                    if name == f"vara{h}":
                        bank, done = full(act, it, 1, f"vara{h}")
                        n = mark(act.activation(rs1[:, cols(h)], bank, ACT.Ln, bias=eps_col))
                        act.activation(rs2[:, cols(h)], bank, ACT.Ln, scale=1.0 + EPS,
                                       bias=eps2_col).then_inc(done, 1)
                        after(n)
                        mark(act.activation(rs1[:, cols(h)], rs1[:, cols(h)], ACT.Exp, scale=-0.5))
                        was_read(act, it, 1, f"vara{h}")
                        act.activation(rs2[:, cols(h)], rs2[:, cols(h)], ACT.Exp, scale=-0.5).then_inc(stds_a.sem, 1)
                    if name == f"k{h}":
                        for key, to, n in (("k", xc, 0), ("v", rs1, 1)):
                            bank, done = full(act, it, 1, f"{key}{h}")
                            act.activation(to[:, cols(h)], bank, ACT.Identity, bias=fold[:, n:n + 1]).then_inc(done, 1)
                        gate_parts(it, "r", h, 2, rs2, relu_r).then_inc(gate_r_ready.sem, 1)
                    if name == "cenf0":
                        centered(it, 1, f"cenf{h}", h, xc, rs1)
                    if name == "varf0":
                        inverse_stds(it, 1, f"varf{h}", h, rs1, stds_f.sem)
                    if name.startswith(f"up{h}"):
                        for use in names:
                            k = int(use[-1])
                            bank, done = full(act, it, 1, use)
                            act.activation(hidden[:, 4 * h + k, :], bank, ACT.Relu,
                                           bias=fold[:, 4 + k % 2:5 + k % 2]).then_inc(done, 1)
                        for use in names:
                            k = int(use[-1])
                            was_read(act, it, 1, use)
                            act.activation(hidden[:, 4 * h + k, :], hidden[:, 4 * h + k, :],
                                           ACT.Square).then_inc(hidden_ready.sem, 1)
                    if name == "gate0":
                        n = mark(gate_parts(it, "gate", h, 3, rs2, relu_r))
                        after(n)
                        act.activation(rs2[:, cols(h)], rs2[:, cols(h)], ACT.Ln,
                                       bias=one_col).then_inc(gate_log.sem, 1)

            def update_exponentials(it):
                act.wait_ge(diff_ready.sem, diff_ready.at(it, 1))
                n = mark(act.activation(wide[:, 2, :], hn[:, :], ACT.Relu, bias=decay[:, 3:4]))
                m = mark(act.activation(wide[:, 3, :], hn[:, :], ACT.Relu, bias=decay[:, 2:3], scale=-1.0))
                after(n)
                mark(act.activation(wide[:, 2, :], wide[:, 2, :], ACT.Exp, scale=-1.0))
                after(m)
                act.activation(wide[:, 3, :], wide[:, 3, :], ACT.Exp, scale=-1.0).then_inc(update_gates.sem, 1)

            def output_exponentials(it):
                n = mark(act.activation(wide[:, 0, :], hn[:, :], ACT.Relu))
                m = mark(act.activation(wide[:, 1, :], hn[:, :], ACT.Relu, scale=-1.0))
                after(n)
                mark(act.activation(wide[:, 0, :], wide[:, 0, :], ACT.Exp, scale=-1.0))
                after(m)
                act.activation(wide[:, 1, :], wide[:, 1, :], ACT.Exp, scale=-1.0).then_inc(output_gates.sem, 1)

            def mixed_log(it):
                act.wait_ge(quotient_log_arg.sem, quotient_log_arg.at(it, 1))
                act.activation(hn[:, :], hn[:, :], ACT.Ln).then_inc(quotient_log.sem, 1)

            def mixed_quotient(it):
                act.wait_ge(quotient_exp_arg.sem, quotient_exp_arg.at(it, 1))
                act.activation(hn[:, :], hn[:, :], ACT.Exp, scale=-1.0).then_inc(quotient.sem, 1)

            def gate(it):
                act.wait_ge(gate_exp_arg.sem, gate_exp_arg.at(it, 1))
                act.activation(rs2[:, :], rs2[:, :], ACT.Exp, scale=-1.0).then_inc(gate_ready.sem, 1)

            def part2(it, names):
                run, name = it - 1, names[0]
                for h in range(2):
                    if name == "cenm0":
                        act.wait_ge(written.sem, written.at(run, 0))
                        centered(it, 2, f"cenm{h}", h, xm, rm)
                    if name == "varm0":
                        inverse_stds(it, 2, f"varm{h}", h, rm, stds_m.sem)
                    if name == "one0":
                        bank, done = full(act, it, 2, f"one{h}")
                        act.activation(choice_t[:, cols(h)], bank, ACT.Copy)
                        act.activation(others_t[:, cols(h)], bank, ACT.Identity, bias=minus1_col).then_inc(done, 1)
                    if name.startswith(f"mu{h}"):
                        for use in names:
                            k = int(use[-1])
                            bank, done = full(act, it, 2, use)
                            at = V_MB1 + k % BLOCKS
                            act.activation(moe_hidden[:, k, :], bank, ACT.Relu,
                                           bias=v_sb[:, at:at + 1]).then_inc(done, 1)
                    if name == f"out{h}":
                        bank, done = full(act, it, 2, f"out{h}")
                        act.activation(rm[:, cols(h)], bank, ACT.Copy).then_inc(done, 1)

            def iteration(it):
                parts = parts_of(it)
                for j in range(SLOTS):
                    if j % 4 == 2:
                        if j >= 4 and samples_in(it):
                            exponentials(it, j // 4 - 1)
                        elif j < 4 and 1 in parts and not (isinstance(it, int) and it == 0):
                            exponentials(it - 1, TILES - 1)
                    if samples_in(it) and j % 2 == 0:
                        copy_points(it, j // 2)
                    for part, names in stages(it, j):
                        if part == 1:
                            part1(it, names)
                        elif part == 2:
                            part2(it, names)
                        else:
                            prepare(it, part, names[0])
                    for b in range(2):
                        if f"q{b}" in parts:
                            if j == SCALAR_AT[f"feature_std{b}"]:
                                inverse_std(it, b)
                            if j == SCALAR_AT[f"gelu_exp{b}"]:
                                gelu_exponential(it, b)
                    if "q0" in parts and j == COMMIT_AT[0]:
                        commit_queries(it + 1, 0)
                    if samples_in(it) and j == COMMIT_AT[1]:
                        commit_queries(it, 1)
                    if 1 in parts and j == SCALAR_AT["update"]:
                        update_exponentials(it)
                    if 1 in parts and j == SCALAR_AT["output"]:
                        output_exponentials(it)
                    if 1 in parts:
                        if j == SCALAR_AT["mixed_log"]:
                            mixed_log(it)
                        if j == SCALAR_AT["mixed_quotient"]:
                            mixed_quotient(it)
                        if j == SCALAR_AT["gate"]:
                            gate(it)

            for b in range(2):
                for _, part, names in SCHEDULE:
                    if part == f"q{b}":
                        prepare(-1, part, names[0])
                        if names[0] == "qo0":
                            inverse_std(-1, b)
                            gelu_exponential(-1, b)
                if b == 0:
                    commit_queries(0, 0)
            all_iterations(act, iteration, scalar_steps)

        @block.vector
        def _(dve):
            def mark(ins):
                return vector_steps.mark(ins)

            def after(n):
                dve.wait_ge(vector_steps.sem, vector_steps.value(n))

            def step(ins):
                after(mark(ins))

            def rows(at, n, shape):
                return v_sb[:, at:at + n].unsqueeze(1).broadcast_to(shape)

            mark(dve.memset(eps_col, EPS))
            mark(dve.memset(eps2_col, EPS * EPS))
            mark(dve.memset(minus1_col, -1.0))
            mark(dve.memset(one_col, 1.0))
            mark(dve.memset(image_base[:, :], 0.0))
            mark(dve.memset(choice[:, :, :], 0.0))
            mark(dve.memset(state_o[:, 0:1], -1e38))
            mark(dve.memset(state_p[:, 0:1], 0.0))
            mark(dve.memset(state_q[:, 0:1], 0.0))
            dve.wait_ge(loaded.sem, 16 * 5)
            step(dve.tensor_scalar(decay[:, 0:1], v_sb[:, V_W:V_W + 1], 1.0 / SEQ, None, ALU.mult))
            step(dve.tensor_scalar(decay[:, 1:2], v_sb[:, V_U:V_U + 1], 1.0 / SEQ, None, ALU.mult))
            step(dve.tensor_tensor(decay[:, 2:3], decay[:, 0:1], decay[:, 1:2], ALU.add))
            step(dve.tensor_scalar(decay[:, 3:4], decay[:, 2:3], -1.0, None, ALU.mult))
            dve.wait_ge(bias_read.sem, 1)
            step(dve.tensor_scalar(w_sb[:, W_K:W_R + 1, :], w_sb[:, W_K:W_R + 1, :], v_sb[:, V_G1:V_G1 + 1],
                                   None, ALU.mult))
            step(dve.tensor_scalar(w_sb[:, W_UP:W_UP + 4, :], w_sb[:, W_UP:W_UP + 4, :],
                                   v_sb[:, V_G2:V_G2 + 1], None, ALU.mult))
            dve.tensor_scalar(w_sb[:, W_FR, :], w_sb[:, W_FR, :], v_sb[:, V_G2:V_G2 + 1],
                              None, ALU.mult).then_inc(folded.sem, 1)
            dve.wait_ge(folded.sem, 1)
            dve.sem_inc(filled.sem, 1)

            def grid_corners(it, b):
                dve.wait_ge(grid_loaded.sem, grid_loaded.at(it + 1, 16 * (b + 1)))
                px = grid_px[:, :, :].rearrange("p t (k c) -> p (t k) c", c=C)
                wt = s_sb[:, S_GW:S_GW + 4 * TILES].unsqueeze(2).broadcast_to([P, 4 * TILES, C])
                step(dve.tensor_tensor(px, px, wt, ALU.mult))
                px = grid_px[:, :, :]
                dve.tensor_tensor(px[:, :, 0:2 * C], px[:, :, 0:2 * C], px[:, :, 2 * C:4 * C], ALU.add).then_inc(grid_summed.sem, 1)

            def features(it, b):
                part, shape = f"q{b}", [P, TILES, OFF]
                was_read(dve, it, part, "qo0")
                was_read(dve, it, part, "qo1")
                step(dve.tensor_tensor(feat_a[:, :, :], qo_tmp[:, :, C:C + OFF], rows(V_BO1, OFF, shape), ALU.add))
                step(dve.tensor_reduce(feat_s[:, 0, :], feat_a[:, :, :], AX_X, ALU.add))
                step(dve.tensor_scalar(feat_s[:, 0, :], feat_s[:, 0, :], 1.0 / OFF, None, ALU.mult))
                step(dve.tensor_tensor(feat_a[:, :, :], feat_a[:, :, :],
                                       feat_s[:, 0, :].unsqueeze(2).broadcast_to(shape), ALU.subtract))
                step(dve.tensor_tensor(feat_b[:, :, :], feat_a[:, :, :], feat_a[:, :, :], ALU.mult))
                dve.tensor_reduce(feat_s[:, 1, :], feat_b[:, :, :], AX_X, ALU.add).then_inc(feature_var.sem, 1)

            def normalised(it, b):
                shape = [P, TILES, OFF]
                dve.wait_ge(feature_std.sem, feature_std.at(it + 1, b + 1))
                step(dve.tensor_tensor(feat_b[:, :, :], feat_a[:, :, :],
                                       feat_r[:, 1, :].unsqueeze(2).broadcast_to(shape), ALU.mult))
                step(dve.tensor_tensor(feat_b[:, :, :], feat_b[:, :, :], rows(V_LNG, OFF, shape), ALU.mult))
                step(dve.tensor_tensor(feat_b[:, :, :], feat_b[:, :, :], rows(V_LNB, OFF, shape), ALU.add))
                step(dve.tensor_tensor(feat_a[:, :, :], feat_b[:, :, :], feat_b[:, :, :], ALU.mult))
                step(dve.tensor_scalar(feat_a[:, :, :], feat_a[:, :, :], 0.044715, 1.0, ALU.mult, ALU.add))
                dve.tensor_tensor(feat_a[:, :, :], feat_a[:, :, :], feat_b[:, :, :], ALU.mult).then_inc(gelu_arg.sem, 1)

            def gelu(it, b):
                dve.wait_ge(gelu_exp.sem, gelu_exp.at(it + 1, b + 1))
                step(dve.tensor_scalar(feat_c[:, :, :], feat_c[:, :, :], 1.0, None, ALU.add))
                step(dve.reciprocal(feat_c[:, :, :], feat_c[:, :, :]))
                dve.tensor_tensor(feat_b[:, :, :], feat_b[:, :, :], feat_c[:, :, :], ALU.mult).then_inc(gelu_ready.sem, 1)

            def sampling_points(it, b):
                bank, done = full(dve, it, f"q{b}", "of")
                off = bank[:, 0:P].rearrange("p (t f) -> p t f", t=TILES)
                dve.tensor_tensor(feat_a[:, :, :], off, rows(V_BO2, OFF, [P, TILES, OFF]), ALU.add).then_inc(done, 1)
                was_read(dve, it, f"q{b}", "of")
                base = s_sb[:, S_BASE:S_BASE + P]
                step(dve.scalar_tensor_tensor(
                    frac[:, :, :, :].rearrange("p t h x -> p (t h x)"),
                    feat_a[:, :, :].rearrange("p t f -> p (t f)"), 4.0, base, ALU.mult, ALU.add))
                step(dve.tensor_scalar(frac[:, :, :, :], frac[:, :, :, :], 0.0, SIDE - 1.0, ALU.max, ALU.min))
                step(dve.tensor_scalar(corner[:, :, :, :], frac[:, :, :, :], -0.5, 0.0, ALU.add, ALU.max))
                step(dve.tensor_scalar(corner[:, :, :, :], corner[:, :, :, :], ROUND, None, ALU.add))
                step(dve.tensor_scalar(corner[:, :, :, :], corner[:, :, :, :], -ROUND, SIDE - 2.0, ALU.add, ALU.min))
                step(dve.tensor_tensor(frac[:, :, :, :], frac[:, :, :, :], corner[:, :, :, :], ALU.subtract))

            def commit_points(it, b):
                away = feat_c[:, :, :].rearrange("p t (h x) -> p t h x", x=2)
                flat = feat_a[:, :, 0:HEADS]
                a = mark(dve.tensor_scalar(away, frac[:, :, :, :], -1.0, 1.0, ALU.mult, ALU.add))
                n = mark(dve.scalar_tensor_tensor(flat, corner[:, :, :, 0], float(SIDE), corner[:, :, :, 1],
                                                  ALU.mult, ALU.add))
                after(n)
                dve.tensor_scalar(index[:, b, :].rearrange("p (t h) -> p t h", t=TILES), flat,
                                  image_base[:, 0:1], None, ALU.add).then_inc(index_ready.sem, 1)
                for x in range(2):
                    for y in range(2):
                        wx = (away, frac[:, :, :, :])[x][:, :, :, 0]
                        wy = (away, frac[:, :, :, :])[y][:, :, :, 1]
                        n = mark(dve.tensor_tensor(mix[:, b, :, :, 2 * y + x], wx, wy, ALU.mult))
                dve.wait_ge(index_ready.sem, index_ready.at(it, b + 1))
                step(dve.tensor_scalar(image_base[:, :], image_base[:, :], float(IMAGE_ROWS), None, ALU.add))

            def weigh(it, n):
                b, t, s = n // TILES, n % TILES, n % RING
                dve.wait_ge(slot_gathered[s].sem, slot_gathered[s].at(it, (n // RING + 1) * HEADS * 16))
                g = gathered[:, s, :].rearrange("p (k c) -> p k c", c=C)
                wt = mix[:, b, t, :, :].rearrange("p h k -> p (h k)").unsqueeze(2).broadcast_to([P, 4 * HEADS, C])
                step(dve.tensor_tensor(g, g, wt, ALU.mult))
                g = gathered[:, s, :].rearrange("p (k n) -> p k n", k=HEADS)
                dve.tensor_tensor(g[:, :, 0:2 * C], g[:, :, 0:2 * C], g[:, :, 2 * C:4 * C], ALU.add).then_inc(weighted.sem, 1)

            kv = kv_ps[:, :, :].rearrange("p a (k n) -> p (a k) n", k=4)

            def score(it, m):
                b, t = m // (TILES // 2), 2 * m % TILES
                shape = [P, 2, HEADS, HEADS]
                dve.wait_ge(kv_full.sem, kv_full.at(it, 4 * m + 4))
                dve.wait_ge(queries_ready.sem, queries_ready.at(it, b + 1))
                step(dve.tensor_tensor(products[:, :, :, :], kv[:, :, 0:C].rearrange("p (t k) n -> p t k n", t=2),
                                       queries[:, b, t:t + 2, :].unsqueeze(2).broadcast_to([P, 2, HEADS, C]),
                                       ALU.mult))
                step(dve.tensor_reduce(scores[:, :, :, :].rearrange("p t k h -> p (t k h)"),
                                       products[:, :, :, :].rearrange("p t k (h d) -> p (t k h) d", h=HEADS),
                                       AX_X, ALU.add))
                step(dve.tensor_reduce(top[:, :, :], scores[:, :, :, :].rearrange("p t k h -> p t h k"),
                                       AX_X, ALU.max))
                dve.tensor_tensor(shifted[:, :, :, :], scores[:, :, :, :],
                                  top[:, :, :].unsqueeze(2).broadcast_to(shape),
                                  ALU.subtract).then_inc(scores_ready.sem, 1)

            def attend(it, m):
                b, t = m // (TILES // 2), 2 * m % TILES
                dve.wait_ge(probs_ready.sem, probs_ready.at(it, m + 1))
                dve.tensor_tensor(products[:, :, :, :].rearrange("p t k (h d) -> p (t k) h d", h=HEADS),
                                  kv[:, :, C:2 * C].rearrange("p k (h d) -> p k h d", h=HEADS),
                                  probs[:, :, :, :].rearrange("p t k h -> p (t k) h").unsqueeze(3).broadcast_to(
                                      [P, 2 * HEADS, HEADS, DH]), ALU.mult).then_inc(values_used.sem, 1)
                n = mark(dve.tensor_reduce(prob_sum[:, :, :], probs[:, :, :, :].rearrange("p t k h -> p t h k"),
                                           AX_X, ALU.add))
                dve.wait_ge(values_used.sem, values_used.at(it, m + 1))
                mark(dve.tensor_reduce(attended_raw[:, :, :], products[:, :, :, :].rearrange("p t k c -> p t c k"),
                                       AX_X, ALU.add))
                after(n)
                step(dve.reciprocal(prob_sum[:, :, :], prob_sum[:, :, :]))
                if t % 4 == 0 and b == 0:
                    was_read(dve, it, 1, f"in{t // 4}")
                dve.tensor_tensor(attended[:, t:t + 2, b, :].rearrange("p t (h d) -> p t h d", h=HEADS),
                                  attended_raw[:, :, :].rearrange("p t (h d) -> p t h d", h=HEADS),
                                  prob_sum[:, :, :].unsqueeze(3).broadcast_to([P, 2, HEADS, DH]),
                                  ALU.mult).then_inc(attended_ready.sem, 1)

            def mix_input(it, h):
                dve.wait_ge(stds_a.sem, stds_a.at(it, h + 1))
                mark(dve.tensor_tensor(x1[:, cols(h)], xc[:, cols(h)], rs1[:, cols(h)], ALU.mult))
                dve.tensor_tensor(hn[:, cols(h)], xc[:, cols(h)], rs2[:, cols(h)], ALU.mult).then_inc(mix_in_ready.sem, 1)

            def running_max(it):
                for key in ("k1", "v1"):
                    was_read(dve, it, 1, key)
                dve.wait_ge(gate_r_ready.sem, gate_r_ready.at(it, 2))
                step(dve.tensor_tensor_scan(state_o[:, 1:NQ + 1], decay[:, 0:1].broadcast_to([P, NQ]), xc[:, :],
                                            state_o[:, 0:1], ALU.add, ALU.max))
                dve.scalar_tensor_tensor(hn[:, :], xc[:, :], decay[:, 1:2], state_o[:, 0:NQ],
                                         ALU.add, ALU.subtract).then_inc(diff_ready.sem, 1)

            def running_sums(it):
                dve.wait_ge(diff_ready.sem, diff_ready.at(it, 1))
                dve.wait_ge(update_gates.sem, update_gates.at(it, 1))
                n = mark(dve.tensor_tensor(xc[:, :], wide[:, 3, :], rs1[:, :], ALU.mult))
                mark(dve.tensor_tensor_scan(state_q[:, 1:NQ + 1], wide[:, 2, :], wide[:, 3, :],
                                            state_q[:, 0:1], ALU.mult, ALU.add))
                after(n)
                step(dve.tensor_tensor_scan(state_p[:, 1:NQ + 1], wide[:, 2, :], xc[:, :],
                                            state_p[:, 0:1], ALU.mult, ALU.add))

            def mixed_sums(it):
                dve.wait_ge(output_gates.sem, output_gates.at(it, 1))
                a = mark(dve.tensor_tensor(hn[:, :], wide[:, 0, :], state_q[:, 0:NQ], ALU.mult))
                b = mark(dve.tensor_tensor(rs1[:, :], wide[:, 1, :], rs1[:, :], ALU.mult))
                c = mark(dve.tensor_tensor(wide[:, 0, :], wide[:, 0, :], state_p[:, 0:NQ], ALU.mult))
                after(a)
                d = mark(dve.tensor_tensor(hn[:, :], hn[:, :], wide[:, 1, :], ALU.add))
                after(c)
                mark(dve.tensor_tensor(wide[:, 0, :], wide[:, 0, :], rs1[:, :], ALU.add))
                after(d)
                dve.scalar_tensor_tensor(hn[:, :], rs2[:, :], 1.0, hn[:, :],
                                         ALU.add, ALU.mult).then_inc(quotient_log_arg.sem, 1)

            def mixed_exponent(it):
                dve.wait_ge(quotient_log.sem, quotient_log.at(it, 1))
                dve.tensor_tensor(hn[:, :], hn[:, :], relu_r[:, :], ALU.add).then_inc(quotient_exp_arg.sem, 1)

            def mixed(it):
                dve.wait_ge(quotient.sem, quotient.at(it, 1))
                dve.tensor_tensor(wide[:, 0, :], wide[:, 0, :], hn[:, :], ALU.mult).then_inc(mixed_ready.sem, 1)
                if isinstance(it, int) and it == 0:
                    for state in (state_o, state_p, state_q):
                        step(dve.tensor_copy(state[:, 0:1], state[:, 1:2]))

            def add_mix(it):
                for h in range(2):
                    bank, done = full(dve, it, 1, f"wo{h}")
                    dve.tensor_tensor(x1[:, cols(h)], x1[:, cols(h)], bank, ALU.add).then_inc(done, 1)

            def ffn_input(it):
                for h in range(2):
                    dve.wait_ge(stds_f.sem, stds_f.at(it, h + 1))
                    dve.tensor_tensor(hn[:, cols(h)], xc[:, cols(h)], rs1[:, cols(h)],
                                      ALU.mult).then_inc(ffn_in_ready.sem, 1)

            def gate_exponent(it):
                dve.wait_ge(gate_log.sem, gate_log.at(it, 2))
                dve.tensor_tensor(rs2[:, :], rs2[:, :], relu_r[:, :], ALU.add).then_inc(gate_exp_arg.sem, 1)

            def add_ffn(it, h):
                dve.wait_ge(gate_ready.sem, gate_ready.at(it, 1))
                bank, done = full(dve, it, 1, f"dn{h}")
                dve.tensor_tensor(rs2[:, cols(h)], bank, rs2[:, cols(h)], ALU.mult).then_inc(done, 1)
                was_read(dve, it, 1, f"dn{h}")
                step(dve.tensor_tensor(x1[:, cols(h)], x1[:, cols(h)], rs2[:, cols(h)], ALU.add))
                dve.tensor_tensor(hm[:, cols(h)], h0[:, cols(h)], x1[:, cols(h)], ALU.add).then_inc(hm_ready.sem, 1)

            def moe_input(it):
                for h in range(2):
                    dve.wait_ge(stds_m.sem, stds_m.at(it - 1, h + 1))
                    dve.tensor_tensor(nm[:, cols(h)], xm[:, cols(h)], rm[:, cols(h)],
                                      ALU.mult).then_inc(nm_ready.sem, 1)

            def take_logits(it):
                for h in range(2):
                    bank, done = full(dve, it, 2, f"route{h}")
                    dve.tensor_tensor(
                        logits[:, 4 * h:4 * h + 4, :, :],
                        bank.rearrange("p (t b e) -> p t b e", t=4, b=4)[:, :, 0:2, :],
                        v_sb[:, V_RB:V_RB + EXPERTS].unsqueeze(1).unsqueeze(1).broadcast_to([P, 4, 2, EXPERTS]),
                        ALU.add).then_inc(done, 1)

            def choose(it):
                shape = [P, 2 * TILES, EXPERTS]
                flat = logits[:, :, :, :].rearrange("p t b e -> p (t b) e")
                most = logit_top[:, :, :].rearrange("p t b -> p (t b)")
                ranks = s_sb[:, S_RANK:S_RANK + EXPERTS].unsqueeze(1).broadcast_to(shape)
                for h in range(2):
                    was_read(dve, it, 2, f"route{h}")
                step(dve.tensor_reduce(most, flat, AX_X, ALU.max))
                step(dve.tensor_tensor(flat, flat, most.unsqueeze(2).broadcast_to(shape), ALU.is_equal))
                step(dve.tensor_tensor(flat, flat, ranks, ALU.mult))
                step(dve.tensor_reduce(most, flat, AX_X, ALU.max))
                dve.tensor_tensor(choice[:, :, 0:2 * EXPERTS].rearrange("p t (b e) -> p t b e", b=2),
                                  logits[:, :, :, :],
                                  logit_top[:, :, :].unsqueeze(3).broadcast_to([P, TILES, 2, EXPERTS]),
                                  ALU.is_equal).then_inc(choice_ready.sem, 1)

            def add_moe(it, h):
                bank, done = full(dve, it, 2, f"md{h}")
                dve.scalar_tensor_tensor(xm[:, cols(h)], bank, 0.0, hm[:, cols(h)], ALU.max, ALU.add).then_inc(done, 1)

            def iteration(it):
                parts = parts_of(it)
                first = isinstance(it, int) and it == 0
                for j in range(SLOTS):
                    if samples_in(it) and j % 2 == 0:
                        weigh(it, j // 2)
                    stage = {1: score, 3: attend}.get(j % 4)
                    if stage and j >= 4 and samples_in(it):
                        stage(it, j // 4 - 1)
                    elif stage and j < 4 and 1 in parts and not first:
                        stage(it - 1, TILES - 1)
                    for b in range(2):
                        if f"q{b}" in parts:
                            for name, stage in (("grid_corners", grid_corners), ("features", features),
                                                ("normalised", normalised), ("gelu", gelu),
                                                ("sampling_points", sampling_points)):
                                if j == VECTOR_AT[f"{name}{b}"]:
                                    stage(it, b)
                    if "q0" in parts and j == COMMIT_AT[0]:
                        commit_points(it + 1, 0)
                    if samples_in(it) and j == COMMIT_AT[1]:
                        commit_points(it, 1)
                    if 1 in parts:
                        for h in range(2):
                            if j == VECTOR_AT[f"mix_input{h}"]:
                                mix_input(it, h)
                            if j == VECTOR_AT[f"add_ffn{h}"]:
                                add_ffn(it, h)
                        if j == VECTOR_AT["running_max"]:
                            running_max(it)
                        if j == VECTOR_AT["running_sums"]:
                            running_sums(it)
                        if j == VECTOR_AT["mixed_sums"]:
                            mixed_sums(it)
                        if j == VECTOR_AT["mixed_exponent"]:
                            mixed_exponent(it)
                        if j == VECTOR_AT["mixed"]:
                            mixed(it)
                        if j == VECTOR_AT["add_mix"]:
                            add_mix(it)
                        if j == VECTOR_AT["ffn_input"]:
                            ffn_input(it)
                        if j == VECTOR_AT["gate_exponent"]:
                            gate_exponent(it)
                    if 2 in parts:
                        if j == VECTOR_AT["moe_input"]:
                            moe_input(it)
                        if j == VECTOR_AT["take_logits"]:
                            take_logits(it)
                        if j == VECTOR_AT["choose"]:
                            choose(it)
                        for h in range(2):
                            if j == VECTOR_AT[f"add_moe{h}"]:
                                add_moe(it, h)

            for b in range(2):
                grid_corners(-1, b)
                features(-1, b)
                normalised(-1, b)
                gelu(-1, b)
                sampling_points(-1, b)
                if b == 0:
                    commit_points(0, 0)
            all_iterations(dve, iteration, vector_steps)


def _padded(blocks, rows=P, cols=P):
    m = np.zeros((rows, cols), np.float32)
    for r, c, a in blocks:
        m[r:r + a.shape[0], c:c + a.shape[1]] = a
    return m


def _weight_matrices(i):
    wq, wk, wv = i["L0_tok_W_q"].T, i["L0_tok_W_k"].T, i["L0_tok_W_v"].T
    twice = lambda a: _padded([(0, 0, a), (a.shape[0], a.shape[1], a)])
    ms = [None] * N_WEIGHTS
    ms[W_KV] = _padded([(r, c, a) for r in (0, C) for c, a in ((0, wk), (C, wv))])
    ms[W_QO] = _padded([(r, c, a) for r in (0, C) for c, a in ((0, wq), (C, i["L0_tok_W_o1"]))])
    ms[W_O2] = _padded([(OFF * t, OFF * t, i["L0_tok_W_o2"]) for t in range(TILES)])
    for m, name in ((W_K, "Wk"), (W_V, "Wv"), (W_R, "Wr"), (W_O, "Wo"), (W_FR, "Wr_ffn")):
        ms[m] = twice(i["L0_attn_" + name])
    ms[W_RT] = twice(i["L0_ffn_router_w"].T)
    ms[W_B2] = twice(i["L0_ffn_b2"])
    up = i["L0_ffn_W1"].transpose(1, 0, 2).reshape(C, EXPERTS * EH)
    down = i["L0_ffn_W2"].reshape(EXPERTS * EH, C)
    for b in range(2):
        for m in range(2):
            part = slice(m * P, (m + 1) * P)
            ms[W_UP + 2 * b + m] = _padded([(b * C, 0, i["L0_attn_Wk_ffn"][:, part])])
            ms[W_DN + 2 * b + m] = _padded([(0, b * C, i["L0_attn_Wv_ffn"][part])])
        for m in range(BLOCKS):
            part = slice(m * P, (m + 1) * P)
            ms[W_MU + BLOCKS * b + m] = _padded([(b * C, 0, up[:, part])])
            ms[W_MD + BLOCKS * b + m] = _padded([(0, b * C, down[part])])
    return np.ascontiguousarray(np.stack(ms, axis=1))


def _vectors(i):
    m = np.zeros((P, N_VECTORS), np.float32)
    for at, name in ((V_G1, "g1"), (V_B1, "b1"), (V_G2, "g2"), (V_B2, "b2"), (V_U, "spatial_first"),
                     (V_W, "spatial_decay")):
        m[0:C, at] = m[C:2 * C, at] = i["L0_attn_" + name]
    m[:, V_MB1:V_MB1 + BLOCKS] = i["L0_ffn_b1"].reshape(BLOCKS, P).T
    for at, name in ((V_BO1, "L0_tok_b_o1"), (V_LNG, "L0_tok_ln_g"), (V_LNB, "L0_tok_ln_b"),
                     (V_BO2, "L0_tok_b_o2"), (V_RB, "L0_ffn_router_b")):
        m[:, at:at + i[name].shape[0]] = i[name]
    return m


def _consts():
    m = np.zeros((P, N_CONSTS, P), np.float32)
    eye = np.eye(P, dtype=np.float32)
    mean = _padded([(r, r, np.full((C, C), 1.0 / C, np.float32)) for r in (0, C)])
    m[:, C_IDENT], m[:, C_CENTER], m[:, C_MEAN] = eye, eye - mean, mean
    for b in range(2):
        for k in range(BLOCKS):
            for e in range(EXPERTS // BLOCKS):
                row = EXPERTS * b + EXPERTS // BLOCKS * k + e
                m[row, C_SEL + BLOCKS * b + k, EH * e:EH * (e + 1)] = MASKED
    return m


def _grid_positions():
    x = (np.linspace(-1.0, 1.0, GRID).astype(np.float32) + 1.0) * 0.5 * (SIDE - 1)
    x0 = np.clip(np.floor(x), 0, SIDE - 2)
    return x.astype(np.float32), x0.astype(np.int64), np.clip(x - x0, 0.0, 1.0).astype(np.float32)


def _shape_vectors():
    x, _, w = _grid_positions()
    q = np.arange(NQ)
    gy, gx = q // GRID, q % GRID
    wx = np.stack([1 - w[gx], w[gx]], 1)
    wy = np.stack([1 - w[gy], w[gy]], 1)
    corners = (wy[:, :, None] * wx[:, None, :]).reshape(TILES, P, 4)
    base = np.tile(np.stack([x[gx], x[gy]], 1), HEADS).reshape(TILES, P, 2 * HEADS)
    m = np.zeros((P, N_SHAPE_VECTORS), np.float32)
    m[:, S_GW:S_GW + 4 * TILES] = corners.transpose(1, 0, 2).reshape(P, -1)
    m[:, S_BASE:S_RANK] = base.transpose(1, 0, 2).reshape(P, -1)
    m[:, S_RANK:] = EXPERTS - np.arange(EXPERTS)
    return m


def kernel(**inputs):
    import concourse.bacc as _bacc
    from concourse.bass_utils import run_bass_kernel_spmd as _run

    i = {name: np.asarray(a) for name, a in inputs.items()}
    x = i["x"]
    images = x.shape[0]
    last = x.transpose(0, 3, 2, 1)
    paired = np.empty((images, SIDE - 1, SIDE, 2, C), x.dtype)
    paired[:, :, :, 0] = last[:, :-1]
    paired[:, :, :, 1] = last[:, 1:]
    _, x0, _ = _grid_positions()
    grid = paired[:, x0][:, :, x0[:, None] + np.arange(2)].transpose(0, 2, 1, 3, 4, 5)
    grid = grid.reshape(images, TILES, P, PATCH).transpose(0, 2, 1, 3).reshape(images, P, TILES * PATCH)
    arrays = {
        "pixels": paired.reshape(images * IMAGE_ROWS, 2 * C),
        "grid": np.ascontiguousarray(grid),
        "cls": np.ascontiguousarray(np.broadcast_to(i["cls_tok"].reshape(1, C), (P, C))),
        "weights": _weight_matrices(i),
        "vectors": _vectors(i),
        "consts": _consts(),
        "shape_vectors": _shape_vectors(),
    }
    nc = _bacc.Bacc("TRN2", target_bir_lowering=False, num_devices=1)
    args = [nc.dram_tensor(n, a.shape, mybir.dt.from_np(a.dtype), kind="ExternalInput").ap()
            for n, a in arrays.items()]
    out = nc.dram_tensor("out", (images, SEQ, C), F32, kind="ExternalOutput").ap()
    vit_kernel(nc, *args, out)
    return _run(nc, [arrays], core_ids=[0]).results[0]["out"]
```
